# Optimizing a Trainium2 kernel written in Bass

```python
import numpy as np
import jax
import jax.numpy as jnp

def _softmax(x, axis=-1):
    return jax.nn.softmax(x, axis=axis)
def _gelu(x):
    return jax.nn.gelu(x, approximate=True)
def _silu(x):
    return jax.nn.silu(x)
def _sigmoid(x):
    return jax.nn.sigmoid(x)
def _layernorm(x, axis=-1, eps=1e-5):
    m = jnp.mean(x, axis=axis, keepdims=True)
    v = jnp.var(x, axis=axis, keepdims=True)
    return (x - m) / jnp.sqrt(v + eps)
def _scatter_add(tgt, idx, src, axis=0):
    return tgt.at[idx].add(src)
def _segment_sum(src, seg, n):
    return jax.ops.segment_sum(src, seg, n)

kernel_name = 'mk_conv_preact_d1_conv_nchw128_fff1d3'

def setup_inputs(seed: int = 0):
    np.random.seed(seed)
    _w = jnp.asarray
    def _rec_inputs():
        import jax
        import jax.numpy as jnp
        _gk = jax.random.key(seed)
        x = -0.0003972 + 0.9999 * jax.random.normal(jax.random.fold_in(_gk, 1), (64, 128, 64, 25), jnp.float32)
        return x
    x = _rec_inputs()
    def _L0_conv_setup():
        import jax, jax.numpy as jnp
        import numpy as np
        N_HEAD = 8
        key = jax.random.key(seed)
        ks = jax.random.split(key, 5)
        N, C, T, V = (64, 128, 64, 25)
        x = jax.random.normal(ks[0], (N, C, T, V), dtype=jnp.float32)
        Wa = jax.random.normal(ks[1], (C, C), dtype=jnp.float32) * (1.0 / np.sqrt(C))
        ba = jax.random.normal(ks[2], (C,), dtype=jnp.float32) * 0.01
        Wp = jax.random.normal(ks[3], (C, C), dtype=jnp.float32) * (1.0 / np.sqrt(C))
        bp = jax.random.normal(ks[4], (C,), dtype=jnp.float32) * 0.01
        temp = jnp.ones((N_HEAD, 1), dtype=jnp.float32)
        denom_bias = jnp.zeros((N_HEAD, 1, 1), dtype=jnp.float32)
        return {'x': x, 'Wa': Wa, 'ba': ba, 'Wp': Wp, 'bp': bp, 'temp': temp, 'denom_bias': denom_bias}
    _L0_conv_all = _L0_conv_setup()
    _L0_conv_in = {k: v for k, v in _L0_conv_all.items() if k in ('Wa', 'ba', 'Wp', 'bp', 'temp', 'denom_bias', )}
    del _L0_conv_all

    return {
        "x": x,
        "L0_conv_Wa": _L0_conv_in["Wa"],
        "L0_conv_ba": _L0_conv_in["ba"],
        "L0_conv_Wp": _L0_conv_in["Wp"],
        "L0_conv_bp": _L0_conv_in["bp"],
        "L0_conv_temp": _L0_conv_in["temp"],
        "L0_conv_denom_bias": _L0_conv_in["denom_bias"],
    }

def reference(x, L0_conv_Wa, L0_conv_ba, L0_conv_Wp, L0_conv_bp, L0_conv_temp, L0_conv_denom_bias):
    import jax
    import jax.numpy as jnp
    def _L0_conv_ref(x, Wa, ba, Wp, bp, temp, denom_bias):
        import jax, jax.numpy as jnp
        import numpy as np
        N_HEAD = 8
        N, C, T, V = x.shape
        H = N_HEAD
        hd = C // H
        res = x
        w = jnp.einsum('nctv,oc->notv', x, Wa) + ba[None, :, None, None]
        w = w.reshape(N, H, hd, T, V).transpose(0, 1, 3, 4, 2).reshape(N, H, T * V, hd)
        w_sq = w * w
        denom = jnp.maximum(jnp.cumsum(w_sq, axis=2), 1e-12)
        w_normed = w_sq / denom + denom_bias
        tmp = jnp.sum(w_normed, axis=-1) * temp
        Pi = jax.nn.softmax(tmp, axis=2)
        dots = jnp.cumsum(w_sq * Pi[..., None], axis=2) / (jnp.cumsum(Pi, axis=2) + 1e-08)[..., None]
        attn = 1.0 / (1.0 + dots)
        y = -(w * Pi[..., None]) * attn
        y = y.reshape(N, H, T, V, hd).transpose(0, 1, 4, 2, 3).reshape(N, C, T, V)
        y = jnp.einsum('nctv,oc->notv', y, Wp) + bp[None, :, None, None]
        y = y + res
        return jax.nn.relu(y)

    def _gn(v, G=32, eps=1e-5):
        B_, C_, H_, W_ = v.shape
        g = v.reshape(B_, G, C_ // G, H_, W_)
        m = jnp.mean(g, axis=(2, 3, 4), keepdims=True)
        s = jnp.var(g, axis=(2, 3, 4), keepdims=True)
        return ((g - m) / jnp.sqrt(s + eps)).reshape(v.shape)

    def _ln_c(v, eps=1e-6):
        m = jnp.mean(v, axis=1, keepdims=True)
        s = jnp.var(v, axis=1, keepdims=True)
        return (v - m) / jnp.sqrt(s + eps)

    def _ln_t(v, eps=1e-5):
        m = jnp.mean(v, axis=-1, keepdims=True)
        s = jnp.var(v, axis=-1, keepdims=True)
        return (v - m) / jnp.sqrt(s + eps)

    def _to_tokens(v):
        B_, C_, H_, W_ = v.shape
        return v.reshape(B_, C_, H_ * W_).transpose(0, 2, 1)
    def _from_tokens(t, like):
        B_, C_, H_, W_ = like.shape
        return t.transpose(0, 2, 1).reshape(B_, C_, H_, W_)

    x = x + _L0_conv_ref(_gn(x), L0_conv_Wa, L0_conv_ba, L0_conv_Wp, L0_conv_bp, L0_conv_temp, L0_conv_denom_bias)
    return x


_drawn_inputs = setup_inputs


def setup_inputs(seed=0):
    import zlib

    import numpy as np

    out = dict(_drawn_inputs(seed))
    spreads = {'L0_conv_temp': (1.0, 0.6), 'L0_conv_denom_bias': (0.0, 2.0)}
    factors = {'L0_conv_Wa': 25.622, 'L0_conv_ba': 200.0, 'L0_conv_Wp': 25.876, 'L0_conv_bp': 8.0}
    for name, (base, spread) in spreads.items():
        noise = np.random.default_rng([zlib.crc32(name.encode()), seed]).standard_normal(out[name].shape)
        drawn = base * np.exp(spread * noise) if base else spread * noise
        out[name] = jnp.asarray(drawn.astype(out[name].dtype))
    for name, factor in factors.items():
        out[name] = (out[name] * factor).astype(out[name].dtype)
    return out
```

```python
import concourse.bass as bass
from concourse import mybir
from contextlib import ExitStack

N, C, T, V = 64, 128, 64, 25
TV = T * V
HEADS, GROUPS = 8, 32
HD = C // HEADS
BATCH, QUARTERS = 4, 4
Q = TV // QUARTERS
HALF = TV // 2
RING = 8
STAT, WIDE, HEAD, SCAN, PROJ = 0, 1, 2, 5, 6
SLOTS = N + PROJ
GN_EPS, CUM_EPS, DENOM_MIN = 1e-5, 1e-8, 1e-12
FLOOR = 2.0 ** -80
LN_SCALE = 2.0 ** -60
MATRICES = ["ident", "group4", "mean_spread", "before", "same", "same_eps", "first_eps", "shift"]
BANK = 512


def pieces(lo, hi):
    out = []
    while lo < hi:
        end = min(hi, (lo // BANK + 1) * BANK)
        out.append((lo, end))
        lo = end
    return out


def conv_preact(nc, x, wa_t, wp_t, chan, rows, mats, sel, pick, group32, out):
    f32 = mybir.dt.float32
    ALU, ACT, AX = mybir.AluOpType, mybir.ActivationFunctionType, mybir.AxisListType
    x_v = x.rearrange("n c t v -> n c (t v)")
    out_v = out.rearrange("n c t v -> n c (t v)")

    with ExitStack() as ctx:
        def sb(name, shape):
            return ctx.enter_context(nc.sbuf_tensor(name, shape, f32))

        def sem(name):
            return ctx.enter_context(nc.semaphore(name))

        xt = [sb(f"x{i}", [C, TV]) for i in range(RING)]
        wt = [sb(f"w{i}", [C, TV]) for i in range(RING)]
        wsq1 = [sb(f"wsq1_{i}", [C, TV]) for i in range(RING)]
        wsq = [sb(f"wsq{i}", [C, TV]) for i in range(2)]
        cum = [sb(f"cum{i}", [C, TV]) for i in range(2)]
        wa_sb, wp_sb = sb("wa", [C, C]), sb("wp", [C, C])
        wa_scaled = [sb(f"wa_scaled{i}", [C, C]) for i in range(2)]
        residual = [sb(f"residual{i}", [C, C]) for i in range(RING)]
        m_sb = sb("mats", [C, len(MATRICES), C])
        mat = {name: m_sb[:, i, :] for i, name in enumerate(MATRICES)}
        sel_sb = sb("sel", [C, BATCH * QUARTERS, C])
        pick_sb = sb("pick", [C, BATCH, 32])
        headw = sb("headw", [C, BATCH, 32])
        group_sb = sb("group32", [C, GROUPS])
        chan_sb = sb("chan", [C, 3])
        rows_sb = sb("rows", [C, 2 + QUARTERS])
        c_row = sb("c_row", [C, 1])
        eps_gn = sb("eps_gn", [C, 1])
        gsum = sb("gsum", [C, RING])
        negm = sb("negm", [C, RING])
        ssq = sb("ssq", [C, RING])
        lvar = sb("lvar", [C, RING])
        rstd = sb("rstd", [C, RING])
        rstd1 = sb("rstd1", [C, RING])
        nmr = sb("nmr", [C, RING])
        bias_w = sb("bias_w", [C, RING])
        bias_o = sb("bias_o", [C, RING])
        E = sb("E", [C, Q])
        Ef = sb("Ef", [C, Q + 1])
        rho = sb("rho", [C, Q])
        D = sb("D", [C, Q])
        Nr = sb("Nr", [C, Q])
        qmax, qmax4, rmax, ebias, esum = (sb("qmax", [C, 1]), sb("qmax4", [C, QUARTERS]), sb("rmax", [C, 1]),
                                          sb("ebias", [C, 1]), sb("esum", [C, 1]))
        sums = sb("sums", [C, 2])
        nrs = sb("nrs", [C, 1])

        units = [ctx.enter_context(nc.psum_tensor(f"unit{i}", [C, 2 * BANK], f32)) for i in range(3)]
        head_ps = ctx.enter_context(nc.psum_tensor("head_ps", [C, BANK], f32))
        stat_ps = ctx.enter_context(nc.psum_tensor("stat_ps", [C, BANK], f32))
        W_UNITS, O_UNITS, R_UNITS, N_UNITS = (0, 1), (2, 0), (1, 2), (0, 1)

        consts_loaded, setup_dve = sem("consts_loaded"), sem("setup_dve")
        x_loaded = [sem(f"x_loaded{i}") for i in range(RING)]
        stored = [sem(f"stored{i}") for i in range(RING)]
        gsum_ps, gsum_done, mean_ps, negm_done = sem("gsum_ps"), sem("gsum_done"), sem("mean_ps"), sem("negm_done")
        ssq_done, var_ps, lvar_done, rstd_done = sem("ssq_done"), sem("var_ps"), sem("lvar_done"), sem("rstd_done")
        nmr_done, bias_o_done, bias_ps, bias_w_done = (sem("nmr_done"), sem("bias_o_done"), sem("bias_ps"),
                                                       sem("bias_w_done"))
        wa_scaled_done, rstd1_done, residual_done = sem("wa_scaled_done"), sem("rstd1_done"), sem("residual_done")
        w_ps, wsq_done, w_done = sem("w_ps"), sem("wsq_done"), sem("w_done")
        cum_done, clamp_done, lncum_done, rcum_done = (sem("cum_done"), sem("clamp_done"), sem("lncum_done"),
                                                       sem("rcum_done"))
        wsq1_done, ratio_done, head_done = sem("wsq1_done"), sem("ratio_done"), sem("head_done")
        qmax_done, qmax4_done, qmax_ps, rmax_done, ebias_done = (sem("qmax_done"), sem("qmax4_done"), sem("qmax_ps"),
                                                                 sem("rmax_done"), sem("ebias_done"))
        e_done, floor_done, sums_ps, sums_done, d_done = (sem("e_done"), sem("floor_done"), sem("sums_ps"),
                                                          sem("sums_done"), sem("d_done"))
        prev_done, nrs_done, neg_done, re_done, rho_done, q_done, n_done = (sem("prev_done"), sem("nrs_done"), sem("neg_done"), sem("re_done"),
                                                                  sem("rho_done"), sem("q_done"), sem("n_done"))
        pool_passed = sem("pool_passed")
        rho_ps, g_done, lng_done, rg_done = sem("rho_ps"), sem("g_done"), sem("lng_done"), sem("rg_done")
        n_ps, wn_done, y_done, o_ps, o_done = sem("n_ps"), sem("wn_done"), sem("y_done"), sem("o_ps"), sem("o_done")

        loads = [(wa_sb, wa_t), (wp_sb, wp_t), (m_sb, mats), (sel_sb, sel), (pick_sb, pick), (group_sb, group32),
                 (chan_sb, chan), (rows_sb, rows)]
        SETUP = 16 * len(loads)

        def halves(h):
            return slice(h * HALF, (h + 1) * HALF)

        def run_slots(eng, slot):
            for k in range(RING):
                slot(k, 0, k, lambda lag, k=k: k - lag >= 0)
            with eng.Fori(1, N // RING) as turn:
                for u in range(RING):
                    slot(turn * RING + u, turn, u, lambda lag: True)
            for k in range(N, SLOTS):
                slot(k, k // RING, k % RING, lambda lag, k=k: k - lag < N)

        def batches(turn, u):
            return turn * (RING // BATCH) + ((u - SCAN) // BATCH + 1)

        block = ctx.enter_context(nc.Block())

        @block.sync
        def _(sp):
            for t, src in loads:
                sp.dma_start(t[:], src).then_inc(consts_loaded, 16)
            for n in range(RING):
                sp.dma_start(xt[n][:, :], x_v[n, :, :]).then_inc(x_loaded[n], 16)

            def store(n, u, turn):
                sp.wait_ge(o_done, (n + 1) * 2)
                sp.dma_start(out_v[n, :, :], xt[u][:, :]).then_inc(stored[u], 16)

            store(0, 0, 0)
            with sp.Fori(0, N // RING - 1) as turn:
                for i in range(1, RING + 1):
                    u = i % RING
                    store(turn * RING + i, u, turn)
                    sp.wait_ge(stored[i - 1], (turn + 1) * 16)
                    sp.dma_start(xt[i - 1][:, :], x_v[turn * RING + (RING + i - 1), :, :]).then_inc(x_loaded[i - 1], 16)
            for n in range(N - RING + 1, N):
                store(n, n % RING, 0)
            for u in range(RING):
                sp.wait_ge(stored[u], 16 * (N // RING))

        @block.tensor
        def _(pe):
            pe.wait_ge(consts_loaded, SETUP)
            pe.wait_ge(setup_dve, 3)

            def slot(k, turn, u, there):
                batch = u % BATCH == SCAN % BATCH and there(SCAN)
                b1 = batches(turn, u)
                if there(HEAD):
                    m, s = k - HEAD, (u - HEAD) % BATCH
                    pe.wait_ge(ratio_done, m + 1)
                    if s == 0 and there(SCAN + 1):
                        pe.wait_ge(n_done, batches(turn, u - 1))
                    for j in range(QUARTERS):
                        last = nc.tensor.matmul(head_ps[32 * j:32 * j + 32, 0:Q], headw[:, s, :],
                                                cum[(u - HEAD) % 2][:, j * Q:(j + 1) * Q],
                                                start=(s == 0), stop=(s == BATCH - 1), skip_group_check=True)
                    last.then_inc(head_done, 1)
                if there(WIDE):
                    m = k - WIDE
                    pe.wait_ge(wa_scaled_done, m + 1)
                    for h in range(2):
                        if there(SCAN + 1):
                            pe.wait_ge(wn_done, 2 * (k - SCAN - 1) + h + 1)
                        for lo, hi in pieces(0, HALF):
                            last = nc.tensor.matmul(units[W_UNITS[h]][:, lo:hi], wa_scaled[(u - WIDE) % 2][:, :],
                                                    xt[(u - WIDE) % RING][:, h * HALF + lo:h * HALF + hi],
                                                    start=True, stop=True)
                        last.then_inc(w_ps, 1)
                if batch:
                    pe.wait_ge(qmax4_done, b1)
                    nc.tensor.matmul(head_ps[:, Q:Q + QUARTERS], mat["same"], qmax4[:, :],
                                     start=True, stop=True, skip_group_check=True).then_inc(qmax_ps, 1)
                if there(PROJ):
                    m = k - PROJ
                    pe.wait_ge(residual_done, m + 1)
                    for h in range(2):
                        if h == 0 and there(SCAN + 1):
                            pe.wait_ge(g_done, 2 * (k - SCAN - 1) + 2)
                        if h == 1 and there(WIDE):
                            pe.wait_ge(w_done, 2 * (k - WIDE) + 1)
                        for lo, hi in pieces(0, HALF):
                            ps = units[O_UNITS[h]][:, lo:hi]
                            cut = slice(h * HALF + lo, h * HALF + hi)
                            nc.tensor.matmul(ps, residual[(u - PROJ) % RING][:, :], xt[(u - PROJ) % RING][:, cut],
                                             start=True, stop=False)
                            if h == 0 and lo == 0:
                                pe.wait_ge(y_done, m + 1)
                            last = nc.tensor.matmul(ps, wp_sb[:, :], wt[(u - PROJ) % RING][:, cut],
                                                    start=False, stop=True)
                        last.then_inc(o_ps, 1)
                if batch:
                    pe.wait_ge(floor_done, b1)
                    col = head_ps[:, Q + 4:Q + 5]
                    nc.tensor.matmul(col, mat["before"], esum[:, :], start=True, stop=False, skip_group_check=True)
                    nc.tensor.matmul(col, mat["same_eps"], esum[:, :], start=False, stop=True, skip_group_check=True)
                    nc.tensor.matmul(head_ps[:, Q + 5:Q + 6], mat["same"], esum[:, :], start=True, stop=True,
                                     skip_group_check=True)
                    col = head_ps[:, Q + 6:Q + 7]
                    nc.tensor.matmul(col, mat["shift"], Ef[:, Q:Q + 1], start=True, stop=False, skip_group_check=True)
                    nc.tensor.matmul(col, mat["first_eps"], esum[:, :], start=False, stop=True,
                                     skip_group_check=True).then_inc(sums_ps, 1)
                if there(STAT):
                    pe.wait_ge(x_loaded[u], (turn + 1) * 16)
                    if there(STAT + 1):
                        pe.wait_ge(bias_w_done, k)
                    for j in range(QUARTERS):
                        last = nc.tensor.matmul(stat_ps[32 * j:32 * j + 32, 0:Q], group_sb[:, :],
                                                xt[u][:, j * Q:(j + 1) * Q], start=True, stop=True,
                                                skip_group_check=True)
                    last.then_inc(gsum_ps, 1)
                    pe.wait_ge(gsum_done, k + 1)
                    nc.tensor.matmul(stat_ps[:, Q:Q + 1], mat["mean_spread"], gsum[:, u:u + 1], start=True,
                                     stop=True, skip_group_check=True).then_inc(mean_ps, 1)

                def spread(rows_t, rows_sem, done_sem, unit_of, free):
                    s = (u - SCAN) % BATCH
                    pe.wait_ge(rows_sem, batches(turn, u))
                    for h in range(2):
                        free(h)
                        for j in (2 * h, 2 * h + 1):
                            for lo, hi in pieces((j % 2) * Q, (j % 2 + 1) * Q):
                                at = lo - (j % 2) * Q
                                last = nc.tensor.matmul(units[unit_of[h]][:, lo:hi], sel_sb[:, s * QUARTERS + j, :],
                                                        rows_t[:, at:at + hi - lo], start=True, stop=True,
                                                        skip_group_check=True)
                        last.then_inc(done_sem, 1)

                if there(SCAN):
                    def free(h):
                        if h == 0:
                            if there(WIDE):
                                pe.wait_ge(w_done, 2 * (k - WIDE) + 2)
                        elif there(PROJ):
                            pe.wait_ge(o_done, 2 * (k - PROJ) + 1)
                    spread(rho, rho_done, rho_ps, R_UNITS, free)
                if there(STAT):
                    pe.wait_ge(ssq_done, k + 1)
                    nc.tensor.matmul(stat_ps[:, Q + 1:Q + 2], mat["group4"], ssq[:, u:u + 1], start=True,
                                     stop=True, skip_group_check=True).then_inc(var_ps, 1)
                if there(SCAN):
                    def free(h):
                        if h == 0:
                            if there(PROJ):
                                pe.wait_ge(o_done, 2 * (k - PROJ) + 2)
                        else:
                            pe.wait_ge(g_done, 2 * (k - SCAN) + 1)
                    spread(Nr, n_done, n_ps, N_UNITS, free)
                if there(STAT):
                    pe.wait_ge(nmr_done, k + 1)
                    nc.tensor.matmul(stat_ps[:, Q + 2:Q + 3], wa_sb[:, :], nmr[:, u:u + 1], start=True, stop=True,
                                     skip_group_check=True).then_inc(bias_ps, 1)

            run_slots(pe, slot)

        @block.scalar
        def _(act):
            act.wait_ge(setup_dve, 3)

            def slot(k, turn, u, there):
                batch = u % BATCH == SCAN % BATCH and there(SCAN)
                b1 = batches(turn, u)
                if there(WIDE):
                    m, um = k - WIDE, (u - WIDE) % RING
                    act.wait_ge(bias_w_done, m + 1)
                    if there(WIDE + 2):
                        act.wait_ge(head_done, m - 1)
                    if there(PROJ + 1):
                        act.wait_ge(o_ps, 2 * (k - PROJ - 1) + 2)
                    for h in range(2):
                        act.wait_ge(w_ps, 2 * m + h + 1)
                        ps = units[W_UNITS[h]][:, 0:HALF]
                        act.activation(wsq[um % 2][:, halves(h)], ps, ACT.Square,
                                       bias=bias_w[:, um:um + 1]).then_inc(wsq_done, 1)
                        act.activation(wt[um][:, halves(h)], ps, ACT.Identity,
                                       bias=bias_w[:, um:um + 1]).then_inc(w_done, 1)
                if batch:
                    act.wait_ge(ebias_done, b1)
                    act.activation(E[:, :], head_ps[:, 0:Q], ACT.Exp, bias=ebias[:, :],
                                   accum_out=esum[:, :]).then_inc(e_done, 1)
                if there(STAT):
                    act.wait_ge(negm_done, k + 1)
                    act.activation(wsq1[u][:, :], xt[u][:, :], ACT.Square, bias=negm[:, u:u + 1],
                                   accum_out=ssq[:, u:u + 1]).then_inc(ssq_done, 1)
                if there(WIDE):
                    c = cum[(u - WIDE) % 2]
                    act.wait_ge(clamp_done, m + 1)
                    act.activation(c[:, :], c[:, :], ACT.Ln).then_inc(lncum_done, 1)
                    act.wait_ge(lncum_done, m + 1)
                    act.activation(c[:, :], c[:, :], ACT.Exp, scale=-1.0).then_inc(rcum_done, 1)
                if there(STAT):
                    act.wait_ge(var_ps, k + 1)
                    act.activation(lvar[:, u:u + 1], stat_ps[:, Q + 1:Q + 2], ACT.Ln, bias=eps_gn[:, :],
                                   scale=1.0 / (C // GROUPS * TV)).then_inc(lvar_done, 1)
                    act.wait_ge(lvar_done, k + 1)
                    act.activation(rstd[:, u:u + 1], lvar[:, u:u + 1], ACT.Exp, scale=-0.5).then_inc(rstd_done, 1)
                if there(SCAN):
                    m = k - SCAN
                    g = wsq1[(u - SCAN) % RING]
                    act.wait_ge(g_done, 2 * m + 2)
                    act.activation(g[:, :], g[:, :], ACT.Ln, scale=LN_SCALE).then_inc(lng_done, 1)
                    act.wait_ge(lng_done, m + 1)
                    act.activation(g[:, :], g[:, :], ACT.Exp, scale=-1.0).then_inc(rg_done, 1)

            run_slots(act, slot)

        @block.gpsimd
        def _(pool):
            pool.wait_ge(consts_loaded, SETUP)

            def slot(k, turn, u, there):
                if there(WIDE):
                    m, um = k - WIDE, (u - WIDE) % RING
                    pool.wait_ge(wsq_done, 2 * m + 2)
                    pool.sem_inc(pool_passed, 1)
                    pool.tensor_scalar(wsq1[um][:, :], wsq[um % 2][:, :], 1.0, 1.0, ALU.add,
                                       ALU.mult).then_inc(wsq1_done, 1)
                    pool.wait_ge(rcum_done, m + 1)
                    pool.tensor_tensor(cum[um % 2][:, :], cum[um % 2][:, :], wsq[um % 2][:, :],
                                       ALU.mult).then_inc(ratio_done, 1)
                if there(STAT):
                    pool.wait_ge(rstd_done, k + 1)
                    pool.sem_inc(pool_passed, 1)
                    pool.tensor_scalar(wa_scaled[u % 2][:, :], wa_sb[:, :], rstd[:, u:u + 1], 1.0, ALU.mult,
                                       ALU.mult).then_inc(wa_scaled_done, 1)
                    pool.tensor_scalar(rstd1[:, u:u + 1], rstd[:, u:u + 1], 1.0, 1.0, ALU.add,
                                       ALU.mult).then_inc(rstd1_done, 1)
                    pool.wait_ge(rstd1_done, k + 1)
                    pool.sem_inc(pool_passed, 1)
                    pool.tensor_scalar(residual[u][:, :], mat["ident"], rstd1[:, u:u + 1], 1.0, ALU.mult,
                                       ALU.mult).then_inc(residual_done, 1)
                if there(SCAN):
                    m, um = k - SCAN, (u - SCAN) % RING
                    pool.wait_ge(rg_done, m + 1)
                    pool.wait_ge(wn_done, 2 * m + 2)
                    pool.tensor_tensor(wt[um][:, :], wt[um][:, :], wsq1[um][:, :], ALU.mult).then_inc(y_done, 1)

            run_slots(pool, slot)

        @block.vector
        def _(dve):
            dve.wait_ge(consts_loaded, SETUP)
            dve.memset(eps_gn[:, :], GN_EPS).then_inc(setup_dve, 1)
            dve.tensor_scalar(headw[:, :, :], pick_sb[:, :, :], chan_sb[:, 2:3], None, ALU.mult).then_inc(setup_dve, 1)
            dve.tensor_scalar(c_row[:, :], rows_sb[:, 1:2], float(HD), rows_sb[:, 0:1], ALU.mult,
                              ALU.mult).then_inc(setup_dve, 1)
            dve.wait_ge(setup_dve, 3)

            def slot(k, turn, u, there):
                batch = u % BATCH == SCAN % BATCH and there(SCAN)
                b1 = batches(turn, u)

                def project(h):
                    m, um = k - PROJ, (u - PROJ) % RING
                    dve.wait_ge(o_ps, 2 * m + h + 1)
                    x_half = xt[um][:, halves(h)]
                    dve.scalar_tensor_tensor(out=x_half, in0=units[O_UNITS[h]][:, 0:HALF], scalar=bias_o[:, um:um + 1],
                                             in1=x_half, op0=ALU.add, op1=ALU.max).then_inc(o_done, 1)

                if batch:
                    dve.wait_ge(head_done, b1 * BATCH)
                    dve.reduce_max(qmax[:, :], head_ps[:, 0:Q], axis=AX.X).then_inc(qmax_done, 1)
                    dve.wait_ge(qmax_done, b1)
                    dve.tensor_scalar(qmax4[:, :], rows_sb[:, 2:2 + QUARTERS], qmax[:, :], None,
                                      ALU.mult).then_inc(qmax4_done, 1)
                if there(PROJ):
                    project(0)
                if batch:
                    dve.wait_ge(qmax_ps, b1)
                    dve.reduce_max(rmax[:, :], head_ps[:, Q:Q + QUARTERS], axis=AX.X).then_inc(rmax_done, 1)
                    dve.wait_ge(rmax_done, b1)
                    dve.scalar_tensor_tensor(out=ebias[:, :], in0=rmax[:, :], scalar=c_row[:, :], in1=c_row[:, :],
                                             op0=ALU.add, op1=ALU.subtract, reverse1=True).then_inc(ebias_done, 1)
                if there(PROJ):
                    project(1)
                if there(WIDE):
                    m, um = k - WIDE, (u - WIDE) % RING
                    c = cum[um % 2]
                    dve.wait_ge(wsq_done, 2 * m + 2)
                    dve.tensor_tensor_scan(c[:, :], wsq[um % 2][:, :], wsq[um % 2][:, :], 0.0, ALU.add,
                                           ALU.bypass).then_inc(cum_done, 1)
                if batch:
                    dve.wait_ge(e_done, b1)
                    dve.tensor_scalar(Ef[:, 1:Q + 1], E[:, :], FLOOR, None, ALU.max).then_inc(floor_done, 1)
                if there(WIDE):
                    dve.wait_ge(cum_done, m + 1)
                    dve.tensor_scalar(c[:, :], c[:, :], DENOM_MIN, None, ALU.max).then_inc(clamp_done, 1)
                if batch:
                    if there(PROJ):
                        dve.wait_ge(n_ps, 2 * (k - PROJ) + 2)
                    dve.wait_ge(floor_done, b1)
                    dve.reciprocal(rho[:, :], Ef[:, 1:Q + 1]).then_inc(re_done, 1)
                    dve.wait_ge(sums_ps, b1)
                    dve.tensor_copy(sums[:, :], head_ps[:, Q + 4:Q + 6]).then_inc(sums_done, 1)
                    dve.tensor_copy(Ef[:, 0:1], head_ps[:, Q + 6:Q + 7]).then_inc(prev_done, 1)
                    dve.tensor_scalar(Nr[:, :], E[:, :], 1.0 / FLOOR, 1.0, ALU.mult, ALU.min).then_inc(q_done, 1)
                    dve.wait_ge(sums_done, b1)
                    dve.tensor_tensor_scan(D[:, :], E[:, :], E[:, :], sums[:, 0:1], ALU.add,
                                           ALU.bypass).then_inc(d_done, 1)
                    dve.reciprocal(nrs[:, :], sums[:, 1:2]).then_inc(nrs_done, 1)
                    dve.wait_ge(prev_done, b1)
                    dve.wait_ge(re_done, b1)
                    dve.tensor_tensor(rho[:, :], Ef[:, 0:Q], rho[:, :], ALU.mult).then_inc(rho_done, 1)
                if there(STAT):
                    dve.wait_ge(gsum_ps, k + 1)
                    dve.reduce_sum(gsum[:, u:u + 1], stat_ps[:, 0:Q], axis=AX.X).then_inc(gsum_done, 1)
                    dve.wait_ge(mean_ps, k + 1)
                    dve.tensor_scalar(negm[:, u:u + 1], stat_ps[:, Q:Q + 1], -1.0 / (C // GROUPS * TV), None,
                                      ALU.mult).then_inc(negm_done, 1)
                if batch:
                    dve.wait_ge(nrs_done, b1)
                    dve.tensor_scalar(nrs[:, :], nrs[:, :], -LN_SCALE, None, ALU.mult).then_inc(neg_done, 1)
                    dve.wait_ge(neg_done, b1)
                    dve.wait_ge(d_done, b1)
                    dve.wait_ge(q_done, b1)
                    dve.scalar_tensor_tensor(out=Nr[:, :], in0=Nr[:, :], scalar=nrs[:, :], in1=D[:, :],
                                             op0=ALU.mult, op1=ALU.mult).then_inc(n_done, 1)
                if there(SCAN):
                    m, um = k - SCAN, (u - SCAN) % RING
                    g = wsq1[um]
                    dve.wait_ge(wsq1_done, m + 1)
                    for h in range(2):
                        dve.wait_ge(rho_ps, 2 * m + h + 1)
                        if h:
                            dve.wait_ge(g_done, 2 * m + 1)
                        dve.tensor_tensor_scan(g[:, halves(h)], units[R_UNITS[h]][:, 0:HALF], g[:, halves(h)],
                                               g[:, HALF - 1:HALF] if h else 1.0, ALU.mult,
                                               ALU.add).then_inc(g_done, 1)
                if there(STAT):
                    dve.wait_ge(rstd_done, k + 1)
                    dve.tensor_tensor(nmr[:, u:u + 1], negm[:, u:u + 1], rstd[:, u:u + 1], ALU.mult).then_inc(nmr_done, 1)
                    dve.wait_ge(nmr_done, k + 1)
                    dve.tensor_tensor(bias_o[:, u:u + 1], nmr[:, u:u + 1], chan_sb[:, 1:2],
                                      ALU.add).then_inc(bias_o_done, 1)
                if there(SCAN):
                    for h in range(2):
                        dve.wait_ge(n_ps, 2 * m + h + 1)
                        dve.tensor_tensor(wt[um][:, halves(h)], units[N_UNITS[h]][:, 0:HALF], wt[um][:, halves(h)],
                                          ALU.mult).then_inc(wn_done, 1)
                if there(STAT):
                    dve.wait_ge(bias_ps, k + 1)
                    dve.tensor_tensor(bias_w[:, u:u + 1], stat_ps[:, Q + 2:Q + 3], chan_sb[:, 0:1],
                                      ALU.add).then_inc(bias_w_done, 1)

            run_slots(dve, slot)


def kernel(**inputs):
    import numpy as np
    import concourse.bacc as bacc
    from concourse.bass_utils import run_bass_kernel_spmd

    f = np.float32
    c = np.arange(C)
    quarter, sample, head = c // 32, c // HEADS % BATCH, c % HEADS
    same = (sample[:, None] == sample) & (head[:, None] == head)
    made = {
        "ident": c[:, None] == c,
        "group4": c[:, None] // 4 == c // 4,
        "mean_spread": c[:, None] % 32 == c // 4,
        "before": same & (quarter[:, None] < quarter),
        "same": same,
        "same_eps": same * CUM_EPS,
        "first_eps": (same & (quarter[None, :] == 0)) * CUM_EPS,
        "shift": c[:, None] + 32 == c,
    }
    mats = np.stack([made[n].astype(f) for n in MATRICES], axis=1)
    sel = np.zeros((C, BATCH * QUARTERS, C), f)
    for s in range(BATCH):
        for j in range(QUARTERS):
            sel[:, s * QUARTERS + j, :] = (quarter == j)[:, None] & (sample == s)[:, None] & (head[:, None] == c // HD)
    pick = np.zeros((C, BATCH, 32), f)
    for s in range(BATCH):
        pick[:, s, :] = (np.arange(32) // HEADS == s) & (np.arange(32) % HEADS == c[:, None] // HD)
    group32 = (c[:, None] // 4 == np.arange(GROUPS)).astype(f)
    temp = np.asarray(inputs["L0_conv_temp"]).reshape(HEADS)
    denom_bias = np.asarray(inputs["L0_conv_denom_bias"]).reshape(HEADS)
    chan = np.stack([np.asarray(inputs["L0_conv_ba"]), np.asarray(inputs["L0_conv_bp"]), np.repeat(temp, HD)], axis=1)
    rows = np.concatenate([np.tile(temp, C // HEADS)[:, None], np.tile(denom_bias, C // HEADS)[:, None],
                           (quarter[:, None] == np.arange(QUARTERS)).astype(f)], axis=1)
    arrays = {
        "x": np.asarray(inputs["x"]),
        "wa_t": np.ascontiguousarray(np.asarray(inputs["L0_conv_Wa"]).T),
        "wp_t": np.ascontiguousarray(np.asarray(inputs["L0_conv_Wp"]).T),
        "chan": np.ascontiguousarray(chan), "rows": np.ascontiguousarray(rows), "mats": np.ascontiguousarray(mats),
        "sel": sel, "pick": pick, "group32": group32,
    }
    nc = bacc.Bacc("TRN2", target_bir_lowering=False, num_devices=1)
    args = [nc.dram_tensor(f"in_{n}", a.shape, mybir.dt.from_np(a.dtype), kind="ExternalInput").ap() for n, a in arrays.items()]
    args.append(nc.dram_tensor("out", (N, C, T, V), mybir.dt.float32, kind="ExternalOutput").ap())
    conv_preact(nc, *args)
    r = run_bass_kernel_spmd(nc, [{f"in_{n}": a for n, a in arrays.items()}], core_ids=[0])
    return r.results[0]["out"]
```

```python
import concourse.bass as bass
from concourse import mybir
from contextlib import ExitStack

N, C, T, V = 64, 128, 64, 25
TV = T * V
HEADS, GROUPS = 8, 32
HD = C // HEADS
BATCH, QUARTERS, EIGHTHS, PARTS = 2, 4, 8, 3
Q, EI = TV // QUARTERS, TV // EIGHTHS
HALF = TV // 2
RING = 8
STAT, WIDE, HEAD, SOFT, SCAN, PROJ, STORE = 0, 1, 2, 4, 5, 6, 7
SLOTS = N + STORE
GN_EPS, CUM_EPS, DENOM_MIN = 1e-5, 1e-8, 1e-12
FLOOR = 2.0 ** -64
LN_SCALE = 2.0 ** -32
MATRICES = ["ident", "group4", "mean_spread", "before", "same", "same_eps", "first_eps", "shift"]
BANK = 512


def pieces(lo, hi):
    out = []
    while lo < hi:
        end = min(hi, (lo // BANK + 1) * BANK)
        out.append((lo, end))
        lo = end
    return out


def conv_preact(nc, x, wa_t, wp_t, chan, rows, mats, sel, pick, group32, out):
    f32, bf16 = mybir.dt.float32, mybir.dt.bfloat16
    ALU, ACT, AX = mybir.AluOpType, mybir.ActivationFunctionType, mybir.AxisListType
    x_v = x.rearrange("n c t v -> n c (t v)")
    out_v = out.rearrange("n c t v -> n c (t v)")

    with ExitStack() as ctx:
        def sb(name, shape, dtype=f32):
            return ctx.enter_context(nc.sbuf_tensor(name, shape, dtype))

        def sem(name):
            return ctx.enter_context(nc.semaphore(name))

        xt = [sb(f"x{i}", [C, TV]) for i in range(RING)]
        wt = [sb(f"w{i}", [C, TV]) for i in range(RING)]
        wsq1 = [sb(f"wsq1_{i}", [C, TV]) for i in range(RING)]
        wsq = [sb(f"wsq{i}", [C, TV]) for i in range(2)]
        cum = [sb(f"cum{i}", [C, TV]) for i in range(2)]
        wa_sb, wp_sb = sb("wa", [C, C]), sb("wp", [C, C])
        wa_scaled = [sb(f"wa_scaled{i}", [C, C]) for i in range(2)]
        residual = [sb(f"residual{i}", [C, C]) for i in range(RING)]
        m_sb = sb("mats", [C, len(MATRICES), C])
        mat = {name: m_sb[:, i, :] for i, name in enumerate(MATRICES)}
        sel_f = sb("sel_f", [PARTS * 32, 2 * BATCH, C])
        sel_sb = sb("sel", [PARTS * 32, 2 * BATCH, C], bf16)
        pick_sb = sb("pick", [C, 2 * BATCH, 32])
        headw = sb("headw", [C, 2 * BATCH, 32])
        group_sb = sb("group32", [C, GROUPS])
        chan_sb = sb("chan", [C, 3])
        rows_sb = sb("rows", [C, 2 + EIGHTHS])
        c_row = sb("c_row", [C, 1])
        eps_gn = sb("eps_gn", [C, 1])
        gsum = sb("gsum", [C, RING])
        negm = sb("negm", [C, RING])
        ssq = sb("ssq", [C, RING])
        lvar = sb("lvar", [C, RING])
        rstd = sb("rstd", [C, RING])
        rstd1 = sb("rstd1", [C, RING])
        nmr = sb("nmr", [C, RING])
        bias_w = sb("bias_w", [C, RING])
        bias_o = sb("bias_o", [C, RING])
        E = sb("E", [C, EI])
        Ef = sb("Ef", [C, EI + 1])
        D = sb("D", [C, EI])
        spread_f = sb("spread_f", [C, 2, EI])
        rest = sb("rest", [C, 2, EI])
        parts = sb("parts", [C, PARTS, 2 * EI], bf16)
        stack = [sb(f"stack{i}", [PARTS * 32, QUARTERS, 2 * EI], bf16) for i in range(2)]
        rho, Nr = spread_f[:, 0, :], spread_f[:, 1, :]
        qmax, qmax8, rmax, ebias, esum = (sb("qmax", [C, 1]), sb("qmax8", [C, EIGHTHS]), sb("rmax", [C, 1]),
                                          sb("ebias", [C, 1]), sb("esum", [C, 1]))
        sums = sb("sums", [C, 2])
        nrs = sb("nrs", [C, 1])

        units = [ctx.enter_context(nc.psum_tensor(f"unit{i}", [C, 2 * BANK], f32)) for i in range(3)]
        head_ps = ctx.enter_context(nc.psum_tensor("head_ps", [C, BANK], f32))
        stat_ps = ctx.enter_context(nc.psum_tensor("stat_ps", [C, BANK], f32))
        W_UNITS, O_UNIT, R_UNITS, N_UNITS = (0, 1), 2, (0, 1), (0, 1)

        consts_loaded, setup_dve = sem("consts_loaded"), sem("setup_dve")
        x_loaded = [sem(f"x_loaded{i}") for i in range(RING)]
        stored = [sem(f"stored{i}") for i in range(RING)]
        gsum_ps, gsum_done, mean_ps, negm_done = sem("gsum_ps"), sem("gsum_done"), sem("mean_ps"), sem("negm_done")
        ssq_done, var_ps, lvar_done, rstd_done = sem("ssq_done"), sem("var_ps"), sem("lvar_done"), sem("rstd_done")
        nmr_done, bias_o_done, bias_ps, bias_w_done = (sem("nmr_done"), sem("bias_o_done"), sem("bias_ps"),
                                                       sem("bias_w_done"))
        wa_scaled_done, rstd1_done, residual_done = sem("wa_scaled_done"), sem("rstd1_done"), sem("residual_done")
        w_ps, wsq_done, w_done = sem("w_ps"), sem("wsq_done"), sem("w_done")
        cum_done, clamp_done, lncum_done, rcum_done = (sem("cum_done"), sem("clamp_done"), sem("lncum_done"),
                                                       sem("rcum_done"))
        wsq1_done, ratio_done, head_done = sem("wsq1_done"), sem("ratio_done"), sem("head_done")
        qmax_done, qmax8_done, qmax_ps, rmax_done, ebias_done = (sem("qmax_done"), sem("qmax8_done"), sem("qmax_ps"),
                                                                 sem("rmax_done"), sem("ebias_done"))
        e_done, floor_done, sums_ps, sums_done, d_done = (sem("e_done"), sem("floor_done"), sem("sums_ps"),
                                                          sem("sums_done"), sem("d_done"))
        prev_done, nrs_done, neg_done, re_done, rho_done, q_done, n_done = (sem("prev_done"), sem("nrs_done"), sem("neg_done"), sem("re_done"),
                                                                  sem("rho_done"), sem("q_done"), sem("n_done"))
        hi_done, rest_done, mid_done, lo_done = sem("hi_done"), sem("rest_done"), sem("mid_done"), sem("lo_done")
        stacked = [sem("stacked0"), sem("stacked1")]
        pool_passed, sp_passed = sem("pool_passed"), sem("sp_passed")
        rho_ps, g_done, lng_done, rg_done = sem("rho_ps"), sem("g_done"), sem("lng_done"), sem("rg_done")
        n_ps, wn_done, y_done, o_ps, o_done = sem("n_ps"), sem("wn_done"), sem("y_done"), sem("o_ps"), sem("o_done")

        loads = [(wa_sb, wa_t), (wp_sb, wp_t), (m_sb, mats), (sel_f, sel), (pick_sb, pick), (group_sb, group32),
                 (chan_sb, chan), (rows_sb, rows)]
        SETUP = 16 * len(loads)

        def halves(h):
            return slice(h * HALF, (h + 1) * HALF)

        def run_slots(eng, slot, last_turn=N // RING):
            for k in range(RING):
                slot(k, 0, k, lambda lag, k=k: k - lag >= 0)
            with eng.Fori(1, last_turn) as turn:
                for u in range(RING):
                    slot(turn * RING + u, turn, u, lambda lag: True)
            for k in range(last_turn * RING, SLOTS):
                slot(k, k // RING, k % RING, lambda lag, k=k: k - lag < N)

        def batches(turn, u):
            return turn * (RING // BATCH) + ((u - SOFT) // BATCH + 1)

        def softmax_slot(u, there):
            return u % BATCH == 0 and there(SOFT)

        block = ctx.enter_context(nc.Block())

        @block.sync
        def _(sp):
            for t, src in loads:
                sp.dma_start(t[:], src).then_inc(consts_loaded, 16)
            for n in range(RING):
                sp.dma_start(xt[n][:, :], x_v[n, :, :]).then_inc(x_loaded[n], 16)

            def slot(k, turn, u, there):
                if there(STORE):
                    up = (u - STORE) % RING
                    sp.wait_ge(o_done, 2 * (k - STORE) + 2)
                    if not isinstance(k, int) or k + 1 < N:
                        sp.dma_start(xt[up][:, :], x_v[k + 1, :, :]).then_inc(x_loaded[up], 16)
                    sp.dma_start(out_v[k - STORE, :, :], wt[up][:, :]).then_inc(stored[up], 16)
                if softmax_slot(u, there):
                    b1 = batches(turn, u)
                    at = (u // BATCH) % 2
                    if there(STORE):
                        sp.wait_ge(n_ps, 2 * (k - STORE) + 2)
                        sp.sem_inc(sp_passed, 1)
                    for p, done in enumerate((hi_done, mid_done, lo_done)):
                        sp.wait_ge(done, b1)
                        sp.sem_inc(sp_passed, 1)
                        for j in range(QUARTERS):
                            sp.dma_start(stack[at][32 * p:32 * p + 32, j, :],
                                         parts[32 * j:32 * j + 32, p, :]).then_inc(stacked[at], 16)

            run_slots(sp, slot, N // RING - 1)
            for u in range(RING):
                sp.wait_ge(stored[u], 16 * (N // RING))

        @block.tensor
        def _(pe):
            pe.wait_ge(consts_loaded, SETUP)
            pe.wait_ge(setup_dve, 4)

            def slot(k, turn, u, there):
                softmax = softmax_slot(u, there)
                b1 = batches(turn, u)

                def spread(lag, which, done_sem, unit_of, free):
                    s, at = (u - lag) % BATCH, ((u - lag + SOFT) // BATCH) % 2
                    rows_done = QUARTERS * PARTS * 16
                    pe.wait_ge(stacked[at], rows_done * (turn * (RING // BATCH // 2) + ((u - lag) // BATCH // 2 + 1)))
                    for h in range(2):
                        free(h)
                        for odd in range(2):
                            for j in (2 * h, 2 * h + 1):
                                start = (2 * (j % 2) + odd) * EI
                                for lo, hi in pieces(start, start + EI):
                                    src = which * EI + lo - start
                                    last = nc.tensor.matmul(units[unit_of[h]][:, lo:hi],
                                                            sel_sb[:, odd * BATCH + s, :],
                                                            stack[at][:, j, src:src + hi - lo], start=True,
                                                            stop=True, skip_group_check=True)
                        last.then_inc(done_sem, 1)

                def spread_n():
                    def free(h):
                        pe.wait_ge(g_done, 2 * (k - SCAN) + h + 1)
                    spread(SCAN, 1, n_ps, N_UNITS, free)

                def spread_rho():
                    def free(h):
                        if there(WIDE):
                            pe.wait_ge(w_done, 2 * (k - WIDE) + h + 1)
                        else:
                            pe.wait_ge(wn_done, 2 * (k - SCAN - 1) + h + 1)
                    spread(SCAN, 0, rho_ps, R_UNITS, free)

                def wide(h):
                    if h == 0:
                        pe.wait_ge(wa_scaled_done, k - WIDE + 1)
                    if True:
                        if there(SCAN + 1):
                            pe.wait_ge(wn_done, 2 * (k - SCAN - 1) + h + 1)
                        elif there(HEAD):
                            pe.wait_ge(w_done, 2 * (k - HEAD) + h + 1)
                        for lo, hi in pieces(0, HALF):
                            last = nc.tensor.matmul(units[W_UNITS[h]][:, lo:hi], wa_scaled[(u - WIDE) % 2][:, :],
                                                    xt[(u - WIDE) % RING][:, h * HALF + lo:h * HALF + hi],
                                                    start=True, stop=True)
                        last.then_inc(w_ps, 1)

                def project(h):
                    up = (u - PROJ) % RING
                    if h == 0:
                        pe.wait_ge(residual_done, k - PROJ + 1)
                    if h == 1 or there(PROJ + 1):
                        pe.wait_ge(o_done, 2 * (k - PROJ) + h)
                    cuts = pieces(0, HALF)
                    for lo, hi in cuts:
                        nc.tensor.matmul(units[O_UNIT][:, lo:hi], residual[up][:, :],
                                         xt[up][:, h * HALF + lo:h * HALF + hi], start=True, stop=False)
                    if h == 0:
                        pe.wait_ge(y_done, k - PROJ + 1)
                    for lo, hi in cuts:
                        last = nc.tensor.matmul(units[O_UNIT][:, lo:hi], wp_sb[:, :],
                                                wt[up][:, h * HALF + lo:h * HALF + hi], start=False, stop=True)
                    last.then_inc(o_ps, 1)

                def heads():
                    s = (u - HEAD) % BATCH
                    pe.wait_ge(ratio_done, k - HEAD + 1)
                    if s == 0 and there(SOFT):
                        pe.wait_ge(sums_done, b1)
                        pe.wait_ge(prev_done, b1)
                    for odd in range(2):
                        for j in range(QUARTERS):
                            at = (2 * j + odd) * EI
                            last = nc.tensor.matmul(head_ps[32 * j:32 * j + 32, 0:EI],
                                                    headw[:, odd * BATCH + s, :],
                                                    cum[(u - HEAD) % 2][:, at:at + EI],
                                                    start=(s == 0 and odd == 0), stop=(s == BATCH - 1 and odd == 1),
                                                    skip_group_check=True)
                    last.then_inc(head_done, 1)

                def row_max():
                    pe.wait_ge(qmax8_done, b1)
                    nc.tensor.matmul(head_ps[:, EI:EI + EIGHTHS], mat["same"], qmax8[:, :], start=True, stop=True,
                                     skip_group_check=True).then_inc(qmax_ps, 1)

                def row_sums():
                    pe.wait_ge(floor_done, b1)
                    col = head_ps[:, Q:Q + 1]
                    nc.tensor.matmul(col, mat["before"], esum[:, :], start=True, stop=False, skip_group_check=True)
                    nc.tensor.matmul(col, mat["same_eps"], esum[:, :], start=False, stop=True, skip_group_check=True)
                    nc.tensor.matmul(head_ps[:, Q + 1:Q + 2], mat["same"], esum[:, :], start=True, stop=True,
                                     skip_group_check=True)
                    col = head_ps[:, Q + 2:Q + 3]
                    nc.tensor.matmul(col, mat["shift"], Ef[:, EI:EI + 1], start=True, stop=False,
                                     skip_group_check=True)
                    nc.tensor.matmul(col, mat["first_eps"], esum[:, :], start=False, stop=True,
                                     skip_group_check=True).then_inc(sums_ps, 1)

                def group_sums():
                    pe.wait_ge(x_loaded[u], (turn + 1) * 16)
                    if there(STAT + 1):
                        pe.wait_ge(bias_w_done, k)
                    for j in range(QUARTERS):
                        last = nc.tensor.matmul(stat_ps[32 * j:32 * j + 32, 0:Q], group_sb[:, :],
                                                xt[u][:, j * Q:(j + 1) * Q], start=True, stop=True,
                                                skip_group_check=True)
                    last.then_inc(gsum_ps, 1)

                def group_mean():
                    pe.wait_ge(gsum_done, k + 1)
                    nc.tensor.matmul(stat_ps[:, Q:Q + 1], mat["mean_spread"], gsum[:, u:u + 1], start=True,
                                     stop=True, skip_group_check=True).then_inc(mean_ps, 1)

                def group_var():
                    pe.wait_ge(ssq_done, k + 1)
                    nc.tensor.matmul(stat_ps[:, Q + 1:Q + 2], mat["group4"], ssq[:, u:u + 1], start=True,
                                     stop=True, skip_group_check=True).then_inc(var_ps, 1)

                def bias():
                    pe.wait_ge(nmr_done, k + 1)
                    nc.tensor.matmul(stat_ps[:, Q + 2:Q + 3], wa_sb[:, :], nmr[:, u:u + 1], start=True, stop=True,
                                     skip_group_check=True).then_inc(bias_ps, 1)

                if there(STAT):
                    group_sums()
                if there(WIDE):
                    wide(0)
                if there(STAT):
                    group_mean()
                if there(WIDE):
                    wide(1)
                if softmax:
                    row_max()
                if there(PROJ):
                    project(0)
                if there(SCAN):
                    spread_rho()
                if there(STAT):
                    group_var()
                if there(PROJ):
                    project(1)
                if softmax:
                    row_sums()
                if there(STAT):
                    bias()
                if there(HEAD):
                    heads()
                if there(SCAN):
                    spread_n()

            run_slots(pe, slot)

        @block.scalar
        def _(act):
            act.preload_act_table_set("natural_log_exp_and_others")
            act.wait_ge(setup_dve, 4)

            def slot(k, turn, u, there):
                b1 = batches(turn, u)
                m, um = k - WIDE, (u - WIDE) % RING
                c = cum[(u - WIDE) % 2]
                g = wsq1[(u - SCAN) % RING]

                if there(WIDE):
                    act.wait_ge(bias_w_done, m + 1)
                    if there(WIDE + 2):
                        act.wait_ge(ratio_done, m - 1)
                    if there(WIDE + RING):
                        act.wait_ge(stored[um], 16 * (turn + (u - WIDE) // RING))
                    for h in range(2):
                        act.wait_ge(w_ps, 2 * m + h + 1)
                        ps = units[W_UNITS[h]][:, 0:HALF]
                        act.activation(wsq[um % 2][:, halves(h)], ps, ACT.Square,
                                       bias=bias_w[:, um:um + 1]).then_inc(wsq_done, 1)
                        act.activation(wt[um][:, halves(h)], ps, ACT.Identity,
                                       bias=bias_w[:, um:um + 1]).then_inc(w_done, 1)
                if softmax_slot(u, there):
                    act.wait_ge(ebias_done, b1)
                    act.activation(E[:, :], head_ps[:, 0:EI], ACT.Exp, bias=ebias[:, :],
                                   accum_out=esum[:, :]).then_inc(e_done, 1)
                if there(STAT):
                    act.wait_ge(negm_done, k + 1)
                    act.activation(wsq1[u][:, :], xt[u][:, :], ACT.Square, bias=negm[:, u:u + 1],
                                   accum_out=ssq[:, u:u + 1]).then_inc(ssq_done, 1)
                if there(WIDE):
                    act.wait_ge(clamp_done, m + 1)
                    act.activation(c[:, :], c[:, :], ACT.Ln).then_inc(lncum_done, 1)
                if there(STAT):
                    act.wait_ge(var_ps, k + 1)
                    act.activation(lvar[:, u:u + 1], stat_ps[:, Q + 1:Q + 2], ACT.Ln, bias=eps_gn[:, :],
                                   scale=1.0 / (C // GROUPS * TV)).then_inc(lvar_done, 1)
                    act.wait_ge(lvar_done, k + 1)
                    act.activation(rstd[:, u:u + 1], lvar[:, u:u + 1], ACT.Exp, scale=-0.5).then_inc(rstd_done, 1)
                if there(WIDE):
                    act.wait_ge(lncum_done, m + 1)
                    act.activation(c[:, :], c[:, :], ACT.Exp, scale=-1.0).then_inc(rcum_done, 1)
                if there(SCAN):
                    act.wait_ge(g_done, 2 * (k - SCAN) + 2)
                    act.activation(g[:, :], g[:, :], ACT.Ln, scale=LN_SCALE).then_inc(lng_done, 1)
                    act.wait_ge(lng_done, k - SCAN + 1)
                    act.activation(g[:, :], g[:, :], ACT.Exp, scale=-1.0).then_inc(rg_done, 1)

            run_slots(act, slot)

        @block.gpsimd
        def _(pool):
            pool.wait_ge(consts_loaded, SETUP)

            def slot(k, turn, u, there):
                b1 = batches(turn, u)
                if there(PROJ):
                    um = (u - PROJ) % RING
                    pool.wait_ge(rg_done, k - PROJ + 1)
                    pool.wait_ge(wn_done, 2 * (k - PROJ) + 2)
                    pool.tensor_tensor(wt[um][:, :], wt[um][:, :], wsq1[um][:, :], ALU.mult).then_inc(y_done, 1)
                if there(HEAD):
                    c, q = cum[(u - HEAD) % 2], wsq[(u - HEAD) % 2]
                    pool.wait_ge(rcum_done, k - HEAD + 1)
                    pool.tensor_tensor(c[:, :], c[:, :], q[:, :], ALU.mult).then_inc(ratio_done, 1)
                if there(WIDE):
                    um = (u - WIDE) % RING
                    pool.wait_ge(wsq_done, 2 * (k - WIDE) + 2)
                    pool.sem_inc(pool_passed, 1)
                    pool.tensor_scalar(wsq1[um][:, :], wsq[um % 2][:, :], 1.0, 1.0, ALU.add,
                                       ALU.mult).then_inc(wsq1_done, 1)
                if there(STAT):
                    pool.wait_ge(rstd_done, k + 1)
                    pool.sem_inc(pool_passed, 1)
                    pool.tensor_scalar(wa_scaled[u % 2][:, :], wa_sb[:, :], rstd[:, u:u + 1], 1.0, ALU.mult,
                                       ALU.mult).then_inc(wa_scaled_done, 1)
                    pool.tensor_scalar(rstd1[:, u:u + 1], rstd[:, u:u + 1], 1.0, 1.0, ALU.add,
                                       ALU.mult).then_inc(rstd1_done, 1)
                    pool.wait_ge(rstd1_done, k + 1)
                    pool.sem_inc(pool_passed, 1)
                    pool.tensor_scalar(residual[u][:, :], mat["ident"], rstd1[:, u:u + 1], 1.0, ALU.mult,
                                       ALU.mult).then_inc(residual_done, 1)
                if softmax_slot(u, there):
                    both = spread_f[:, :, :].rearrange("p a b -> p (a b)")
                    left = rest[:, :, :].rearrange("p a b -> p (a b)")
                    pool.wait_ge(hi_done, b1)
                    pool.tensor_tensor(left, both, parts[:, 0, :], ALU.subtract).then_inc(rest_done, 1)
                    pool.wait_ge(mid_done, b1)
                    pool.tensor_tensor(parts[:, 2, :], left, parts[:, 1, :], ALU.subtract).then_inc(lo_done, 1)

            run_slots(pool, slot)

        @block.vector
        def _(dve):
            dve.wait_ge(consts_loaded, SETUP)
            dve.memset(eps_gn[:, :], GN_EPS).then_inc(setup_dve, 1)
            dve.tensor_copy(sel_sb[:, :, :], sel_f[:, :, :]).then_inc(setup_dve, 1)
            dve.tensor_scalar(headw[:, :, :], pick_sb[:, :, :], chan_sb[:, 2:3], None, ALU.mult).then_inc(setup_dve, 1)
            dve.tensor_scalar(c_row[:, :], rows_sb[:, 1:2], float(HD), rows_sb[:, 0:1], ALU.mult,
                              ALU.mult).then_inc(setup_dve, 1)
            dve.wait_ge(setup_dve, 4)

            def slot(k, turn, u, there):
                softmax = softmax_slot(u, there)
                b1 = batches(turn, u)
                both = spread_f[:, :, :].rearrange("p a b -> p (a b)")
                left = rest[:, :, :].rearrange("p a b -> p (a b)")
                c = cum[(u - WIDE) % 2]

                def project(h, lag):
                    up = (u - lag) % RING
                    dve.wait_ge(o_ps, 2 * (k - lag) + h + 1)
                    dve.scalar_tensor_tensor(out=wt[up][:, halves(h)], in0=units[O_UNIT][:, 0:HALF],
                                             scalar=bias_o[:, up:up + 1], in1=xt[up][:, halves(h)], op0=ALU.add,
                                             op1=ALU.max).then_inc(o_done, 1)

                def times_n(h):
                    um = (u - SCAN) % RING
                    dve.wait_ge(n_ps, 2 * (k - SCAN) + h + 1)
                    dve.tensor_tensor(wt[um][:, halves(h)], units[N_UNITS[h]][:, 0:HALF], wt[um][:, halves(h)],
                                      ALU.mult).then_inc(wn_done, 1)

                def running_sum(h):
                    q = wsq[(u - WIDE) % 2]
                    dve.wait_ge(wsq_done, 2 * (k - WIDE) + h + 1)
                    if h:
                        dve.wait_ge(cum_done, 2 * (k - WIDE) + 1)
                    elif there(WIDE + 2):
                        dve.wait_ge(head_done, k - WIDE - 1)
                    dve.tensor_tensor_scan(c[:, halves(h)], q[:, halves(h)], q[:, halves(h)],
                                           c[:, HALF - 1:HALF] if h else 0.0, ALU.add,
                                           ALU.bypass).then_inc(cum_done, 1)

                def clamp():
                    dve.wait_ge(cum_done, 2 * (k - WIDE) + 2)
                    dve.tensor_scalar(c[:, :], c[:, :], DENOM_MIN, None, ALU.max).then_inc(clamp_done, 1)

                def scan(h):
                    m, g = k - SCAN, wsq1[(u - SCAN) % RING]
                    if h == 0:
                        dve.wait_ge(wsq1_done, m + 1)
                    dve.wait_ge(rho_ps, 2 * m + h + 1)
                    if h:
                        dve.wait_ge(g_done, 2 * m + 1)
                    dve.tensor_tensor_scan(g[:, halves(h)], units[R_UNITS[h]][:, 0:HALF], g[:, halves(h)],
                                           g[:, HALF - 1:HALF] if h else 1.0, ALU.mult, ALU.add).then_inc(g_done, 1)

                def group_sum():
                    dve.wait_ge(gsum_ps, k + 1)
                    dve.reduce_sum(gsum[:, u:u + 1], stat_ps[:, 0:Q], axis=AX.X).then_inc(gsum_done, 1)

                def group_mean():
                    dve.wait_ge(mean_ps, k + 1)
                    dve.tensor_scalar(negm[:, u:u + 1], stat_ps[:, Q:Q + 1], -1.0 / (C // GROUPS * TV), None,
                                      ALU.mult).then_inc(negm_done, 1)

                def shifts():
                    dve.wait_ge(rstd_done, k + 1)
                    dve.tensor_tensor(nmr[:, u:u + 1], negm[:, u:u + 1], rstd[:, u:u + 1], ALU.mult).then_inc(nmr_done, 1)
                    dve.wait_ge(nmr_done, k + 1)
                    dve.tensor_tensor(bias_o[:, u:u + 1], nmr[:, u:u + 1], chan_sb[:, 1:2],
                                      ALU.add).then_inc(bias_o_done, 1)

                def bias_of_w():
                    dve.wait_ge(bias_ps, k + 1)
                    dve.tensor_tensor(bias_w[:, u:u + 1], stat_ps[:, Q + 2:Q + 3], chan_sb[:, 0:1],
                                      ALU.add).then_inc(bias_w_done, 1)

                def soft_max():
                    dve.wait_ge(head_done, b1 * BATCH)
                    dve.reduce_max(qmax[:, :], head_ps[:, 0:EI], axis=AX.X).then_inc(qmax_done, 1)
                    dve.wait_ge(qmax_done, b1)
                    dve.tensor_scalar(qmax8[:, :], rows_sb[:, 2:2 + EIGHTHS], qmax[:, :], None,
                                      ALU.mult).then_inc(qmax8_done, 1)

                def soft_bias():
                    dve.wait_ge(qmax_ps, b1)
                    dve.reduce_max(rmax[:, :], head_ps[:, EI:EI + EIGHTHS], axis=AX.X).then_inc(rmax_done, 1)
                    dve.wait_ge(rmax_done, b1)
                    dve.scalar_tensor_tensor(out=ebias[:, :], in0=rmax[:, :], scalar=c_row[:, :], in1=c_row[:, :],
                                             op0=ALU.add, op1=ALU.subtract, reverse1=True).then_inc(ebias_done, 1)

                def soft_floor():
                    dve.wait_ge(e_done, b1)
                    dve.tensor_scalar(Ef[:, 1:EI + 1], E[:, :], FLOOR, None, ALU.max).then_inc(floor_done, 1)

                def soft_reciprocal():
                    dve.wait_ge(floor_done, b1)
                    dve.reciprocal(rho, Ef[:, 1:EI + 1]).then_inc(re_done, 1)
                    dve.tensor_scalar(Nr, E[:, :], 1.0 / FLOOR, 1.0, ALU.mult, ALU.min).then_inc(q_done, 1)

                def soft_sums():
                    dve.wait_ge(sums_ps, b1)
                    dve.tensor_copy(sums[:, :], head_ps[:, Q:Q + 2]).then_inc(sums_done, 1)
                    dve.tensor_copy(Ef[:, 0:1], head_ps[:, Q + 2:Q + 3]).then_inc(prev_done, 1)
                    dve.wait_ge(sums_done, b1)
                    dve.reciprocal(nrs[:, :], sums[:, 1:2]).then_inc(nrs_done, 1)
                    dve.tensor_tensor_scan(D[:, :], E[:, :], E[:, :], sums[:, 0:1], ALU.add,
                                           ALU.bypass).then_inc(d_done, 1)
                    dve.wait_ge(nrs_done, b1)
                    dve.tensor_scalar(nrs[:, :], nrs[:, :], -LN_SCALE, None, ALU.mult).then_inc(neg_done, 1)
                    dve.wait_ge(prev_done, b1)
                    dve.wait_ge(re_done, b1)
                    dve.tensor_tensor(rho, Ef[:, 0:EI], rho, ALU.mult).then_inc(rho_done, 1)
                    dve.wait_ge(neg_done, b1)
                    dve.wait_ge(d_done, b1)
                    dve.wait_ge(q_done, b1)
                    dve.scalar_tensor_tensor(out=Nr, in0=Nr, scalar=nrs[:, :], in1=D[:, :], op0=ALU.mult,
                                             op1=ALU.mult).then_inc(n_done, 1)

                def soft_hi():
                    dve.wait_ge(rho_done, b1)
                    dve.wait_ge(n_done, b1)
                    if there(SOFT + BATCH):
                        wait_parts(turn, u)
                    dve.tensor_copy(parts[:, 0, :], both).then_inc(hi_done, 1)

                def soft_mid():
                    dve.wait_ge(rest_done, b1)
                    dve.tensor_copy(parts[:, 1, :], left).then_inc(mid_done, 1)

                def wait_parts(turn, u):
                    last = (u // BATCH - 1) % 2
                    n = turn * (RING // BATCH // 2) + ((u - SOFT - BATCH) // BATCH // 2 + 1)
                    dve.wait_ge(stacked[last], QUARTERS * PARTS * 16 * n)

                if there(STAT):
                    group_sum()
                if softmax:
                    soft_max()
                if there(STORE):
                    project(1, STORE)
                if there(STAT):
                    group_mean()
                if there(WIDE):
                    running_sum(0)
                if softmax:
                    soft_bias()
                if there(WIDE):
                    running_sum(1)
                    clamp()
                if there(PROJ):
                    project(0, PROJ)
                if there(SCAN):
                    scan(0)
                    scan(1)
                if softmax:
                    soft_floor()
                    soft_reciprocal()
                if there(STAT):
                    shifts()
                if softmax:
                    soft_sums()
                    soft_hi()
                    soft_mid()
                if there(STAT):
                    bias_of_w()
                if there(SCAN):
                    times_n(0)
                    times_n(1)

            run_slots(dve, slot)


def kernel(**inputs):
    import numpy as np
    import concourse.bacc as bacc
    from concourse.bass_utils import run_bass_kernel_spmd

    f = np.float32
    c = np.arange(C)
    eighth, sample, head = c // (HEADS * BATCH), c // HEADS % BATCH, c % HEADS
    same = (sample[:, None] == sample) & (head[:, None] == head)
    made = {
        "ident": c[:, None] == c,
        "group4": c[:, None] // 4 == c // 4,
        "mean_spread": c[:, None] % 32 == c // 4,
        "before": same & (eighth[:, None] < eighth),
        "same": same,
        "same_eps": same * CUM_EPS,
        "first_eps": (same & (eighth[None, :] == 0)) * CUM_EPS,
        "shift": c[:, None] + HEADS * BATCH == c,
    }
    mats = np.stack([made[n].astype(f) for n in MATRICES], axis=1)
    r = np.arange(32)
    sel = np.zeros((PARTS * 32, 2 * BATCH, C), f)
    pick = np.zeros((C, 2 * BATCH, 32), f)
    for odd in range(2):
        for s in range(BATCH):
            mine = (r // (HEADS * BATCH) == odd) & (r // HEADS % BATCH == s)
            row_of = mine & (r % HEADS == c[:, None] // HD)
            pick[:, odd * BATCH + s, :] = row_of
            sel[:, odd * BATCH + s, :] = np.tile(row_of.T, (PARTS, 1))
    group32 = (c[:, None] // 4 == np.arange(GROUPS)).astype(f)
    temp = np.asarray(inputs["L0_conv_temp"]).reshape(HEADS)
    denom_bias = np.asarray(inputs["L0_conv_denom_bias"]).reshape(HEADS)
    chan = np.stack([np.asarray(inputs["L0_conv_ba"]), np.asarray(inputs["L0_conv_bp"]), np.repeat(temp, HD)], axis=1)
    rows = np.concatenate([np.tile(temp, C // HEADS)[:, None], np.tile(denom_bias, C // HEADS)[:, None],
                           (eighth[:, None] == np.arange(EIGHTHS)).astype(f)], axis=1)
    arrays = {
        "x": np.asarray(inputs["x"]),
        "wa_t": np.ascontiguousarray(np.asarray(inputs["L0_conv_Wa"]).T),
        "wp_t": np.ascontiguousarray(np.asarray(inputs["L0_conv_Wp"]).T),
        "chan": np.ascontiguousarray(chan), "rows": np.ascontiguousarray(rows), "mats": np.ascontiguousarray(mats),
        "sel": sel, "pick": pick, "group32": group32,
    }
    nc = bacc.Bacc("TRN2", target_bir_lowering=False, num_devices=1)
    args = [nc.dram_tensor(f"in_{n}", a.shape, mybir.dt.from_np(a.dtype), kind="ExternalInput").ap() for n, a in arrays.items()]
    args.append(nc.dram_tensor("out", (N, C, T, V), mybir.dt.float32, kind="ExternalOutput").ap())
    conv_preact(nc, *args)
    r = run_bass_kernel_spmd(nc, [{f"in_{n}": a for n, a in arrays.items()}], core_ids=[0])
    return r.results[0]["out"]
```

```python
import concourse.bass as bass
from concourse import mybir
from contextlib import ExitStack

N, C, T, V = 64, 128, 64, 25
TV = T * V
HEADS, GROUPS = 8, 32
HD = C // HEADS
BATCH, QUARTERS, EIGHTHS, PARTS = 2, 4, 8, 3
Q, EI = TV // QUARTERS, TV // EIGHTHS
HALF = TV // 2
RING = 8
STAT, WIDE, HEAD, SOFT, SCAN, PROJ, STORE = 0, 1, 2, 4, 5, 6, 7
SLOTS = N + STORE
GN_EPS, CUM_EPS, DENOM_MIN = 1e-5, 1e-8, 1e-12
FLOOR = 2.0 ** -64
LN_SCALE = 2.0 ** -32
MATRICES = ["ident", "group4", "mean_spread", "before", "same", "neg_same", "shift"]
BANK = 512


def pieces(lo, hi):
    out = []
    while lo < hi:
        end = min(hi, (lo // BANK + 1) * BANK)
        out.append((lo, end))
        lo = end
    return out


def conv_preact(nc, x, wa_t, wp_t, chan, rows, mats, sel, pick, group32, out):
    f32, bf16 = mybir.dt.float32, mybir.dt.bfloat16
    ALU, ACT, AX = mybir.AluOpType, mybir.ActivationFunctionType, mybir.AxisListType
    x_v = x.rearrange("n c t v -> n c (t v)")
    out_v = out.rearrange("n c t v -> n c (t v)")

    with ExitStack() as ctx:
        def sb(name, shape, dtype=f32):
            return ctx.enter_context(nc.sbuf_tensor(name, shape, dtype))

        def sem(name):
            return ctx.enter_context(nc.semaphore(name))

        xt = [sb(f"x{i}", [C, TV]) for i in range(RING)]
        wt = [sb(f"w{i}", [C, TV]) for i in range(RING)]
        wsq1 = [sb(f"wsq1_{i}", [C, TV]) for i in range(RING)]
        wsq = [sb(f"wsq{i}", [C, TV]) for i in range(2)]
        cum = [sb(f"cum{i}", [C, TV]) for i in range(2)]
        wa_sb, wp_sb = sb("wa", [C, C]), sb("wp", [C, C])
        wa_scaled = [sb(f"wa_scaled{i}", [C, C]) for i in range(2)]
        residual = [sb(f"residual{i}", [C, C]) for i in range(RING)]
        m_sb = sb("mats", [C, len(MATRICES), C])
        mat = {name: m_sb[:, i, :] for i, name in enumerate(MATRICES)}
        sel_f = sb("sel_f", [PARTS * 32, 2 * BATCH, C])
        sel_sb = sb("sel", [PARTS * 32, 2 * BATCH, C], bf16)
        pick_sb = sb("pick", [C, 2 * BATCH, 32])
        headw = sb("headw", [C, 2 * BATCH, 32])
        group_sb = sb("group32", [C, GROUPS])
        chan_sb = sb("chan", [C, 3])
        rows_sb = sb("rows", [C, 2 + EIGHTHS])
        c_row = sb("c_row", [C, 1])
        first_eps = sb("first_eps", [C, 1])
        eps_gn = sb("eps_gn", [C, 1])
        gsum = sb("gsum", [C, RING])
        negm = sb("negm", [C, RING])
        ssq = sb("ssq", [C, RING])
        lvar = sb("lvar", [C, RING])
        rstd = sb("rstd", [C, RING])
        nmr = sb("nmr", [C, RING])
        bias_w = sb("bias_w", [C, RING])
        bias_o = sb("bias_o", [C, RING])
        E = sb("E", [C, EI])
        Ef = sb("Ef", [C, EI + 1])
        D = sb("D", [C, EI])
        spread_f = sb("spread_f", [C, 2, EI])
        rest = sb("rest", [C, 2, EI])
        parts = sb("parts", [C, PARTS, 2 * EI], bf16)
        stack = [sb(f"stack{i}", [PARTS * 32, QUARTERS, 2 * EI], bf16) for i in range(2)]
        rho, Nr = spread_f[:, 0, :], spread_f[:, 1, :]
        qmax, qmax8, rmax, ebias, esum = (sb("qmax", [C, 1]), sb("qmax8", [C, EIGHTHS]), sb("rmax", [C, 1]),
                                          sb("ebias", [C, 1]), sb("esum", [C, 1]))
        d_start = sb("d_start", [C, 1])
        neg_sum = sb("neg_sum", [C, 1])
        nrs = sb("nrs", [C, 1])

        units = [ctx.enter_context(nc.psum_tensor(f"unit{i}", [C, 2 * BANK], f32)) for i in range(3)]
        head_ps = ctx.enter_context(nc.psum_tensor("head_ps", [C, BANK], f32))
        stat_ps = ctx.enter_context(nc.psum_tensor("stat_ps", [C, BANK], f32))

        consts_loaded, setup_dve = sem("consts_loaded"), sem("setup_dve")
        x_loaded = [sem(f"x_loaded{i}") for i in range(RING)]
        stored = [sem(f"stored{i}") for i in range(RING)]
        gsum_ps, gsum_done, mean_ps, negm_done = sem("gsum_ps"), sem("gsum_done"), sem("mean_ps"), sem("negm_done")
        ssq_done, var_ps, lvar_done, rstd_done = sem("ssq_done"), sem("var_ps"), sem("lvar_done"), sem("rstd_done")
        nmr_done, bias_o_done, bias_ps, bias_w_done = (sem("nmr_done"), sem("bias_o_done"), sem("bias_ps"),
                                                       sem("bias_w_done"))
        wa_scaled_done, residual_done = sem("wa_scaled_done"), sem("residual_done")
        w_ps, wsq_done, w_done = sem("w_ps"), sem("wsq_done"), sem("w_done")
        cum_done, clamp_done, lncum_done, rcum_done = (sem("cum_done"), sem("clamp_done"), sem("lncum_done"),
                                                       sem("rcum_done"))
        wsq1_done, ratio_done, head_done = sem("wsq1_done"), sem("ratio_done"), sem("head_done")
        qmax_done, qmax8_done, qmax_ps, rmax_done, ebias_done = (sem("qmax_done"), sem("qmax8_done"), sem("qmax_ps"),
                                                                 sem("rmax_done"), sem("ebias_done"))
        e_done, floor_done, sums_ps, d_start_done, d_done = (sem("e_done"), sem("floor_done"), sem("sums_ps"),
                                                          sem("d_start_done"), sem("d_done"))
        prev_done, nrs_done, re_done, rho_done, q_done, n_done = (sem("prev_done"), sem("nrs_done"), sem("re_done"),
                                                                  sem("rho_done"), sem("q_done"), sem("n_done"))
        neg_sum_done = sem("neg_sum_done")
        hi_done, rest_done, mid_done, lo_done = sem("hi_done"), sem("rest_done"), sem("mid_done"), sem("lo_done")
        stacked = [sem("stacked0"), sem("stacked1")]
        pool_passed, sp_passed = sem("pool_passed"), sem("sp_passed")
        rho_ps, g_done, lng_done, rg_done = sem("rho_ps"), sem("g_done"), sem("lng_done"), sem("rg_done")
        n_ps, wn_done, y_done, o_ps, o_done = sem("n_ps"), sem("wn_done"), sem("y_done"), sem("o_ps"), sem("o_done")

        loads = [(wa_sb, wa_t), (wp_sb, wp_t), (m_sb, mats), (sel_f, sel), (pick_sb, pick), (group_sb, group32),
                 (chan_sb, chan), (rows_sb, rows)]
        SETUP = 16 * len(loads)

        def halves(h):
            return slice(h * HALF, (h + 1) * HALF)

        def run_slots(eng, slot, last_turn=N // RING):
            for k in range(RING):
                slot(k, 0, k, lambda lag, k=k: k - lag >= 0)
            with eng.Fori(1, last_turn) as turn:
                for u in range(RING):
                    slot(turn * RING + u, turn, u, lambda lag: True)
            for k in range(last_turn * RING, SLOTS):
                slot(k, k // RING, k % RING, lambda lag, k=k: k - lag < N)

        def batches(turn, u):
            return turn * (RING // BATCH) + ((u - SOFT) // BATCH + 1)

        block = ctx.enter_context(nc.Block())

        @block.sync
        def _(sp):
            for t, src in loads:
                sp.dma_start(t[:], src).then_inc(consts_loaded, 16)
            for n in range(RING):
                sp.dma_start(xt[n][:, :], x_v[n, :, :]).then_inc(x_loaded[n], 16)

            def slot(k, turn, u, there):
                def store_and_load(lag=STORE):
                    if not there(lag):
                        return
                    up = (u - lag) % RING
                    sp.wait_ge(o_done, 2 * (k - lag) + 2)
                    if not isinstance(k, int) or k - lag + RING < N:
                        sp.dma_start(xt[up][:, :], x_v[k - lag + RING, :, :]).then_inc(x_loaded[up], 16)
                    sp.dma_start(out_v[k - lag, :, :], wt[up][:, :]).then_inc(stored[up], 16)

                def stack_part(p, at_slot=0):
                    if not there(SOFT + at_slot):
                        return
                    b1 = batches(turn, u - at_slot)
                    at = ((u - at_slot) // BATCH) % 2
                    if p == 0 and there(STORE + at_slot):
                        sp.wait_ge(n_ps, 4 * b1 - 8)
                        sp.sem_inc(sp_passed, 1)
                    sp.wait_ge((hi_done, mid_done, lo_done)[p], b1)
                    sp.sem_inc(sp_passed, 1)
                    for j in range(QUARTERS):
                        sp.dma_start(stack[at][32 * p:32 * p + 32, j, :],
                                     parts[32 * j:32 * j + 32, p, :]).then_inc(stacked[at], 16)

                if u % BATCH == 0:
                    store_and_load()
                    stack_part(0)
                else:
                    stack_part(1, at_slot=1)
                    stack_part(2, at_slot=1)
                    store_and_load()

            run_slots(sp, slot, N // RING - 1)
            for u in range(RING):
                sp.wait_ge(stored[u], 16 * (N // RING))

        @block.tensor
        def _(pe):
            pe.wait_ge(consts_loaded, SETUP)
            pe.wait_ge(setup_dve, 5)

            def slot(k, turn, u, there):
                def spread(which, h, done_sem):
                    s, at = (u - SCAN) % BATCH, ((u - SCAN + SOFT) // BATCH) % 2
                    rows_done = QUARTERS * PARTS * 16
                    if h == 0:
                        pe.wait_ge(stacked[at],
                                   rows_done * (turn * (RING // BATCH // 2) + ((u - SCAN) // BATCH // 2 + 1)))
                    for odd in range(2):
                        for j in (2 * h, 2 * h + 1):
                            start = (2 * (j % 2) + odd) * EI
                            for lo, hi in pieces(start, start + EI):
                                src = which * EI + lo - start
                                last = nc.tensor.matmul(units[h][:, lo:hi], sel_sb[:, odd * BATCH + s, :],
                                                        stack[at][:, j, src:src + hi - lo], start=True,
                                                        stop=True, skip_group_check=True)
                    last.then_inc(done_sem, 1)

                def spread_n(h):
                    if there(SCAN):
                        pe.wait_ge(g_done, 2 * (k - SCAN) + h + 1)
                        spread(1, h, n_ps)

                def spread_rho(h):
                    if there(SCAN):
                        if there(WIDE):
                            pe.wait_ge(w_done, 2 * (k - WIDE) + h + 1)
                        else:
                            pe.wait_ge(wn_done, 2 * (k - SCAN - 1) + h + 1)
                        spread(0, h, rho_ps)

                def wide(h):
                    if not there(WIDE):
                        return
                    if h == 0:
                        pe.wait_ge(wa_scaled_done, k - WIDE + 1)
                    if there(SCAN + 1):
                        pe.wait_ge(wn_done, 2 * (k - SCAN - 1) + h + 1)
                    elif there(HEAD):
                        pe.wait_ge(w_done, 2 * (k - HEAD) + h + 1)
                    for lo, hi in pieces(0, HALF):
                        last = nc.tensor.matmul(units[h][:, lo:hi], wa_scaled[(u - WIDE) % 2][:, :],
                                                xt[(u - WIDE) % RING][:, h * HALF + lo:h * HALF + hi],
                                                start=True, stop=True)
                    last.then_inc(w_ps, 1)

                def project(h, lag=PROJ):
                    if not there(lag):
                        return
                    up = (u - lag) % RING
                    if h == 0:
                        pe.wait_ge(residual_done, k - lag + 1)
                    if h == 1 or there(lag + 1):
                        pe.wait_ge(o_done, 2 * (k - lag) + h)
                    cuts = pieces(0, HALF)
                    for lo, hi in cuts:
                        nc.tensor.matmul(units[2][:, lo:hi], residual[up][:, :],
                                         xt[up][:, h * HALF + lo:h * HALF + hi], start=True, stop=False)
                    pe.wait_ge(y_done, 2 * (k - lag) + h + 1)
                    for lo, hi in cuts:
                        last = nc.tensor.matmul(units[2][:, lo:hi], wp_sb[:, :],
                                                wt[up][:, h * HALF + lo:h * HALF + hi], start=False, stop=True)
                    last.then_inc(o_ps, 1)

                def heads():
                    if not there(HEAD):
                        return
                    s = (u - HEAD) % BATCH
                    pe.wait_ge(ratio_done, k - HEAD + 1)
                    if s == 0 and there(SOFT):
                        pe.wait_ge(d_start_done, batches(turn, u))
                    for odd in range(2):
                        for j in range(QUARTERS):
                            at = (2 * j + odd) * EI
                            last = nc.tensor.matmul(head_ps[32 * j:32 * j + 32, 0:EI],
                                                    headw[:, odd * BATCH + s, :],
                                                    cum[(u - HEAD) % 2][:, at:at + EI],
                                                    start=(s == 0 and odd == 0), stop=(s == BATCH - 1 and odd == 1),
                                                    skip_group_check=True)
                    last.then_inc(head_done, 1)

                def row_max(at_slot=0):
                    if not there(SOFT + at_slot):
                        return
                    pe.wait_ge(qmax8_done, batches(turn, u - at_slot))
                    nc.tensor.matmul(head_ps[:, EI:EI + EIGHTHS], mat["same"], qmax8[:, :], start=True, stop=True,
                                     skip_group_check=True).then_inc(qmax_ps, 1)

                def row_sums(at_slot=0):
                    if not there(SOFT + at_slot):
                        return
                    pe.wait_ge(floor_done, batches(turn, u - at_slot))
                    nc.tensor.matmul(head_ps[:, Q:Q + 1], mat["before"], esum[:, :], start=True, stop=True,
                                     skip_group_check=True)
                    nc.tensor.matmul(head_ps[:, Q + 1:Q + 2], mat["neg_same"], esum[:, :], start=True, stop=True,
                                     skip_group_check=True)
                    nc.tensor.matmul(head_ps[:, Q + 2:Q + 3], mat["shift"], Ef[:, EI:EI + 1], start=True, stop=True,
                                     skip_group_check=True).then_inc(sums_ps, 1)

                def group_sums():
                    if not there(STAT):
                        return
                    pe.wait_ge(x_loaded[u], (turn + 1) * 16)
                    if there(STAT + 1):
                        pe.wait_ge(bias_w_done, k)
                    for j in range(QUARTERS):
                        last = nc.tensor.matmul(stat_ps[32 * j:32 * j + 32, 0:Q], group_sb[:, :],
                                                xt[u][:, j * Q:(j + 1) * Q], start=True, stop=True,
                                                skip_group_check=True)
                    last.then_inc(gsum_ps, 1)

                def group_mean():
                    if there(STAT):
                        pe.wait_ge(gsum_done, k + 1)
                        nc.tensor.matmul(stat_ps[:, Q:Q + 1], mat["mean_spread"], gsum[:, u:u + 1], start=True,
                                         stop=True, skip_group_check=True).then_inc(mean_ps, 1)

                def group_var():
                    if there(STAT):
                        pe.wait_ge(ssq_done, k + 1)
                        nc.tensor.matmul(stat_ps[:, Q + 1:Q + 2], mat["group4"], ssq[:, u:u + 1], start=True,
                                         stop=True, skip_group_check=True).then_inc(var_ps, 1)

                def bias():
                    if there(STAT):
                        pe.wait_ge(nmr_done, k + 1)
                        nc.tensor.matmul(stat_ps[:, Q + 2:Q + 3], wa_sb[:, :], nmr[:, u:u + 1], start=True,
                                         stop=True, skip_group_check=True).then_inc(bias_ps, 1)

                drain = isinstance(k, int) and k >= N
                if u % BATCH == 0 and not drain:
                    group_sums()
                    wide(0)
                    wide(1)
                    row_sums()
                    group_mean()
                    project(0)
                    group_var()
                    heads()
                    spread_rho(0)
                    spread_rho(1)
                    project(1)
                    bias()
                    spread_n(0)
                    spread_n(1)
                elif not drain:
                    group_sums()
                    wide(0)
                    group_mean()
                    wide(1)
                    heads()
                    project(0)
                    group_var()
                    spread_rho(0)
                    row_max(at_slot=-1)
                    spread_rho(1)
                    bias()
                    project(1)
                    spread_n(0)
                    spread_n(1)
                elif u % BATCH == 0:
                    wide(0)
                    wide(1)
                    row_sums()
                    project(0)
                    spread_rho(0)
                    spread_rho(1)
                    heads()
                    project(1)
                    spread_n(0)
                    spread_n(1)
                else:
                    wide(0)
                    heads()
                    wide(1)
                    project(0)
                    spread_rho(0)
                    spread_rho(1)
                    row_max(at_slot=-1)
                    spread_n(0)
                    project(1)
                    spread_n(1)

            run_slots(pe, slot)

        @block.scalar
        def _(act):
            act.preload_act_table_set("natural_log_exp_and_others")
            act.wait_ge(setup_dve, 5)

            def slot(k, turn, u, there):
                def exp_heads(at_slot=0):
                    if not there(SOFT + at_slot):
                        return
                    act.wait_ge(ebias_done, batches(turn, u - at_slot))
                    act.activation(E[:, :], head_ps[:, 0:EI], ACT.Exp, bias=ebias[:, :],
                                   accum_out=esum[:, :]).then_inc(e_done, 1)

                def square(h, lag=WIDE):
                    if not there(lag):
                        return
                    m, um = k - lag, (u - lag) % RING
                    if h == 0:
                        act.wait_ge(bias_w_done, m + 1)
                        if there(lag + 2):
                            act.wait_ge(ratio_done, m - 1)
                            act.wait_ge(wsq1_done, m - 1)
                    act.wait_ge(w_ps, 2 * m + h + 1)
                    act.activation(wsq[um % 2][:, halves(h)], units[h][:, 0:HALF], ACT.Square,
                                   bias=bias_w[:, um:um + 1]).then_inc(wsq_done, 1)

                def copy_w(h, lag=WIDE):
                    if not there(lag):
                        return
                    m, um = k - lag, (u - lag) % RING
                    if h == 0:
                        act.wait_ge(bias_w_done, m + 1)
                        if there(lag + RING):
                            act.wait_ge(stored[um], 16 * (turn + (u - lag) // RING))
                    act.wait_ge(w_ps, 2 * m + h + 1)
                    act.wait_ge(wsq_done, 2 * m + h + 1)
                    act.activation(wt[um][:, halves(h)], units[h][:, 0:HALF], ACT.Identity,
                                   bias=bias_w[:, um:um + 1]).then_inc(w_done, 1)

                def deviations():
                    if there(STAT):
                        act.wait_ge(negm_done, k + 1)
                        act.activation(wsq1[u][:, :], xt[u][:, :], ACT.Square, bias=negm[:, u:u + 1],
                                       accum_out=ssq[:, u:u + 1]).then_inc(ssq_done, 1)

                def ln_cum(lag=WIDE):
                    if there(lag):
                        c = cum[(u - lag) % 2]
                        act.wait_ge(clamp_done, k - lag + 1)
                        act.activation(c[:, :], c[:, :], ACT.Ln).then_inc(lncum_done, 1)

                def exp_cum(lag=WIDE):
                    if there(lag):
                        c = cum[(u - lag) % 2]
                        act.wait_ge(lncum_done, k - lag + 1)
                        act.activation(c[:, :], c[:, :], ACT.Exp, scale=-1.0).then_inc(rcum_done, 1)

                def inverse_deviation():
                    if there(STAT):
                        act.wait_ge(var_ps, k + 1)
                        act.activation(lvar[:, u:u + 1], stat_ps[:, Q + 1:Q + 2], ACT.Ln, bias=eps_gn[:, :],
                                       scale=1.0 / (C // GROUPS * TV)).then_inc(lvar_done, 1)
                        act.wait_ge(lvar_done, k + 1)
                        act.activation(rstd[:, u:u + 1], lvar[:, u:u + 1], ACT.Exp, scale=-0.5).then_inc(rstd_done, 1)

                def ln_g(lag=SCAN):
                    if there(lag):
                        g = wsq1[(u - lag) % RING]
                        act.wait_ge(g_done, 2 * (k - lag) + 2)
                        act.activation(g[:, :], g[:, :], ACT.Ln, scale=LN_SCALE).then_inc(lng_done, 1)

                def exp_g(lag=SCAN):
                    if there(lag):
                        g = wsq1[(u - lag) % RING]
                        act.wait_ge(lng_done, k - lag + 1)
                        act.activation(g[:, :], g[:, :], ACT.Exp, scale=-1.0).then_inc(rg_done, 1)

                def group_mean():
                    if there(STAT):
                        act.wait_ge(mean_ps, k + 1)
                        act.mul(negm[:, u:u + 1], stat_ps[:, Q:Q + 1], -1.0 / (C // GROUPS * TV)).then_inc(negm_done, 1)

                def mean_shift():
                    if there(STAT):
                        act.wait_ge(rstd_done, k + 1)
                        act.activation(nmr[:, u:u + 1], negm[:, u:u + 1], ACT.Copy,
                                       scale=rstd[:, u:u + 1]).then_inc(nmr_done, 1)

                def bias_of_w():
                    if there(STAT):
                        act.wait_ge(bias_ps, k + 1)
                        act.activation(bias_w[:, u:u + 1], stat_ps[:, Q + 2:Q + 3], ACT.Identity,
                                       bias=chan_sb[:, 0:1]).then_inc(bias_w_done, 1)

                both = spread_f[:, :, :].rearrange("p a b -> p (a b)")
                left = rest[:, :, :].rearrange("p a b -> p (a b)")

                drain = isinstance(k, int) and k >= N
                if u % BATCH == 0 and not drain:
                    exp_heads()
                    exp_g(lag=PROJ)
                    square(0)
                    copy_w(0)
                    square(1)
                    group_mean()
                    deviations()
                    copy_w(1)
                    ln_cum()
                    inverse_deviation()
                    exp_cum()
                    mean_shift()
                    bias_of_w()
                    ln_g()
                elif not drain:
                    exp_g(lag=PROJ)
                    square(0)
                    copy_w(0)
                    square(1)
                    deviations()
                    copy_w(1)
                    inverse_deviation()
                    mean_shift()
                    ln_cum()
                    exp_cum()
                    ln_g()
                elif u % BATCH == 0:
                    exp_heads()
                    exp_g(lag=PROJ)
                    square(0)
                    square(1)
                    copy_w(0)
                    copy_w(1)
                    ln_cum()
                    exp_cum()
                    ln_g()
                else:
                    exp_g(lag=PROJ)
                    square(0)
                    copy_w(0)
                    copy_w(1)
                    square(1)
                    ln_cum()
                    ln_g()
                    exp_cum()

            run_slots(act, slot)

        @block.gpsimd
        def _(pool):
            pool.wait_ge(consts_loaded, SETUP)

            def slot(k, turn, u, there):
                def y(h, lag=PROJ):
                    if there(lag):
                        um = (u - lag) % RING
                        pool.wait_ge(rg_done, k - lag + 1)
                        pool.wait_ge(wn_done, 2 * (k - lag) + h + 1)
                        y_half = wt[um][:, halves(h)]
                        pool.tensor_tensor(y_half, y_half, wsq1[um][:, halves(h)], ALU.mult).then_inc(y_done, 1)

                def ratio(lag=HEAD):
                    if there(lag):
                        c, q = cum[(u - lag) % 2], wsq[(u - lag) % 2]
                        pool.wait_ge(rcum_done, k - lag + 1)
                        pool.tensor_tensor(c[:, :], c[:, :], q[:, :], ALU.mult).then_inc(ratio_done, 1)

                def one_plus_square(lag=WIDE):
                    if there(lag):
                        um = (u - lag) % RING
                        pool.wait_ge(wsq_done, 2 * (k - lag) + 2)
                        pool.sem_inc(pool_passed, 1)
                        pool.tensor_scalar(wsq1[um][:, :], wsq[um % 2][:, :], 1.0, 1.0, ALU.add,
                                           ALU.mult).then_inc(wsq1_done, 1)

                def scale_wa():
                    if there(STAT):
                        pool.wait_ge(rstd_done, k + 1)
                        pool.sem_inc(pool_passed, 1)
                        pool.tensor_scalar(wa_scaled[u % 2][:, :], wa_sb[:, :], rstd[:, u:u + 1], 1.0, ALU.mult,
                                           ALU.mult).then_inc(wa_scaled_done, 1)

                both = spread_f[:, :, :].rearrange("p a b -> p (a b)")
                left = rest[:, :, :].rearrange("p a b -> p (a b)")

                def rest_part(at_slot=0):
                    if there(SOFT + at_slot):
                        pool.wait_ge(hi_done, batches(turn, u - at_slot))
                        pool.tensor_tensor(left, both, parts[:, 0, :], ALU.subtract).then_inc(rest_done, 1)

                def high_part(at_slot=0):
                    if not there(SOFT + at_slot):
                        return
                    b1 = batches(turn, u - at_slot)
                    pool.wait_ge(rho_done, b1)
                    pool.sem_inc(pool_passed, 1)
                    pool.wait_ge(n_done, b1)
                    pool.sem_inc(pool_passed, 1)
                    if there(SOFT + BATCH + at_slot):
                        at = u - at_slot - BATCH
                        n = turn * (RING // BATCH // 2) + ((at - SOFT) // BATCH // 2 + 1)
                        pool.wait_ge(stacked[at // BATCH % 2], QUARTERS * PARTS * 16 * n)
                        pool.sem_inc(pool_passed, 1)
                    pool.tensor_scalar(parts[:, 0, :], both, 1.0, 1.0, ALU.mult, ALU.mult).then_inc(hi_done, 1)

                def soft_rho(at_slot=0):
                    if not there(SOFT + at_slot):
                        return
                    b1 = batches(turn, u - at_slot)
                    pool.wait_ge(prev_done, b1)
                    pool.wait_ge(re_done, b1)
                    pool.tensor_tensor(rho, Ef[:, 0:EI], rho, ALU.mult).then_inc(rho_done, 1)

                def bias_of_out():
                    if there(STAT):
                        pool.wait_ge(nmr_done, k + 1)
                        pool.tensor_tensor(bias_o[:, u:u + 1], nmr[:, u:u + 1], chan_sb[:, 1:2],
                                           ALU.add).then_inc(bias_o_done, 1)

                drain = isinstance(k, int) and k >= N
                if u % BATCH == 0 and not drain:
                    y(0)
                    one_plus_square()
                    y(1)
                    soft_rho()
                    scale_wa()
                    high_part()
                    rest_part()
                    ratio(lag=WIDE)
                    bias_of_out()
                    y(0, lag=SCAN)
                elif not drain:
                    y(1)
                    bias_of_out()
                    one_plus_square()
                    ratio(lag=WIDE)
                elif u % BATCH == 0:
                    y(0)
                    one_plus_square()
                    soft_rho()
                    y(1)
                    rest_part()
                    ratio(lag=WIDE)
                    y(0, lag=SCAN)
                else:
                    y(1)
                    ratio(lag=WIDE)

            run_slots(pool, slot)

        @block.vector
        def _(dve):
            dve.wait_ge(consts_loaded, SETUP)
            dve.memset(eps_gn[:, :], GN_EPS).then_inc(setup_dve, 1)
            dve.tensor_copy(sel_sb[:, :, :], sel_f[:, :, :]).then_inc(setup_dve, 1)
            dve.tensor_scalar(headw[:, :, :], pick_sb[:, :, :], chan_sb[:, 2:3], None, ALU.mult).then_inc(setup_dve, 1)
            dve.tensor_scalar(c_row[:, :], rows_sb[:, 1:2], float(HD), rows_sb[:, 0:1], ALU.mult,
                              ALU.mult).then_inc(setup_dve, 1)
            dve.tensor_scalar(first_eps[:, :], rows_sb[:, 2:3], -LN_SCALE * CUM_EPS, None,
                              ALU.mult).then_inc(setup_dve, 1)
            dve.wait_ge(setup_dve, 5)

            def slot(k, turn, u, there):
                both = spread_f[:, :, :].rearrange("p a b -> p (a b)")
                left = rest[:, :, :].rearrange("p a b -> p (a b)")

                def final(h, lag=PROJ):
                    if not there(lag):
                        return
                    up = (u - lag) % RING
                    if h == 0:
                        dve.wait_ge(bias_o_done, k - lag + 1)
                    dve.wait_ge(o_ps, 2 * (k - lag) + h + 1)
                    dve.scalar_tensor_tensor(out=wt[up][:, halves(h)], in0=units[2][:, 0:HALF],
                                             scalar=bias_o[:, up:up + 1], in1=xt[up][:, halves(h)], op0=ALU.add,
                                             op1=ALU.max).then_inc(o_done, 1)

                def times_n(h, lag=SCAN):
                    if not there(lag):
                        return
                    um = (u - lag) % RING
                    dve.wait_ge(n_ps, 2 * (k - lag) + h + 1)
                    dve.tensor_tensor(wt[um][:, halves(h)], units[h][:, 0:HALF], wt[um][:, halves(h)],
                                      ALU.mult).then_inc(wn_done, 1)

                def running_sum(h, lag=WIDE):
                    if not there(lag):
                        return
                    q, c = wsq[(u - lag) % 2], cum[(u - lag) % 2]
                    dve.wait_ge(wsq_done, 2 * (k - lag) + h + 1)
                    if h:
                        dve.wait_ge(cum_done, 2 * (k - lag) + 1)
                    elif there(lag + 2):
                        dve.wait_ge(head_done, k - lag - 1)
                    dve.tensor_tensor_scan(c[:, halves(h)], q[:, halves(h)], q[:, halves(h)],
                                           c[:, HALF - 1:HALF] if h else 0.0, ALU.add,
                                           ALU.bypass).then_inc(cum_done, 1)

                def clamp(lag=WIDE):
                    if there(lag):
                        c = cum[(u - lag) % 2]
                        dve.wait_ge(cum_done, 2 * (k - lag) + 2)
                        dve.tensor_scalar(c[:, :], c[:, :], DENOM_MIN, None, ALU.max).then_inc(clamp_done, 1)

                def scan(h, lag=SCAN):
                    if not there(lag):
                        return
                    m, g = k - lag, wsq1[(u - lag) % RING]
                    if h == 0:
                        dve.wait_ge(wsq1_done, m + 1)
                    dve.wait_ge(rho_ps, 2 * m + h + 1)
                    if h:
                        dve.wait_ge(g_done, 2 * m + 1)
                    dve.tensor_tensor_scan(g[:, halves(h)], units[h][:, 0:HALF], g[:, halves(h)],
                                           g[:, HALF - 1:HALF] if h else 1.0, ALU.mult, ALU.add).then_inc(g_done, 1)

                def group_sum():
                    if there(STAT):
                        dve.wait_ge(gsum_ps, k + 1)
                        dve.reduce_sum(gsum[:, u:u + 1], stat_ps[:, 0:Q], axis=AX.X).then_inc(gsum_done, 1)

                def group_mean():
                    if there(STAT):
                        dve.wait_ge(mean_ps, k + 1)
                        dve.tensor_scalar(negm[:, u:u + 1], stat_ps[:, Q:Q + 1], -1.0 / (C // GROUPS * TV), None,
                                          ALU.mult).then_inc(negm_done, 1)

                def bias_of_out():
                    if there(STAT):
                        dve.wait_ge(nmr_done, k + 1)
                        dve.tensor_tensor(bias_o[:, u:u + 1], nmr[:, u:u + 1], chan_sb[:, 1:2],
                                          ALU.add).then_inc(bias_o_done, 1)

                def bias_of_w():
                    if there(STAT):
                        dve.wait_ge(bias_ps, k + 1)
                        dve.tensor_tensor(bias_w[:, u:u + 1], stat_ps[:, Q + 2:Q + 3], chan_sb[:, 0:1],
                                          ALU.add).then_inc(bias_w_done, 1)

                def soft_max(at_slot=0):
                    if not there(SOFT + at_slot):
                        return
                    b1 = batches(turn, u - at_slot)
                    dve.wait_ge(head_done, b1 * BATCH)
                    dve.reduce_max(qmax[:, :], head_ps[:, 0:EI], axis=AX.X).then_inc(qmax_done, 1)
                    dve.wait_ge(qmax_done, b1)
                    dve.tensor_scalar(qmax8[:, :], rows_sb[:, 2:2 + EIGHTHS], qmax[:, :], None,
                                      ALU.mult).then_inc(qmax8_done, 1)

                def soft_bias(at_slot=0):
                    if not there(SOFT + at_slot):
                        return
                    b1 = batches(turn, u - at_slot)
                    dve.wait_ge(qmax_ps, b1)
                    dve.reduce_max(rmax[:, :], head_ps[:, EI:EI + EIGHTHS], axis=AX.X).then_inc(rmax_done, 1)
                    dve.wait_ge(rmax_done, b1)
                    dve.scalar_tensor_tensor(out=ebias[:, :], in0=rmax[:, :], scalar=c_row[:, :], in1=c_row[:, :],
                                             op0=ALU.add, op1=ALU.subtract, reverse1=True).then_inc(ebias_done, 1)

                def soft_floor(at_slot=0):
                    if there(SOFT + at_slot):
                        dve.wait_ge(e_done, batches(turn, u - at_slot))
                        dve.tensor_scalar(Ef[:, 1:EI + 1], E[:, :], FLOOR, None, ALU.max).then_inc(floor_done, 1)

                def soft_quotient(at_slot=0):
                    if there(SOFT + at_slot):
                        dve.wait_ge(e_done, batches(turn, u - at_slot))
                        dve.tensor_scalar(Nr, E[:, :], 1.0 / FLOOR, 1.0, ALU.mult, ALU.min).then_inc(q_done, 1)

                def soft_reciprocal(at_slot=0):
                    if there(SOFT + at_slot):
                        dve.wait_ge(floor_done, batches(turn, u - at_slot))
                        dve.reciprocal(rho, Ef[:, 1:EI + 1]).then_inc(re_done, 1)

                def soft_sums(at_slot=0):
                    if not there(SOFT + at_slot):
                        return
                    b1 = batches(turn, u - at_slot)
                    dve.wait_ge(sums_ps, b1)
                    dve.tensor_copy(neg_sum[:, :], head_ps[:, Q + 1:Q + 2]).then_inc(neg_sum_done, 1)
                    dve.reciprocal(nrs[:, :], head_ps[:, Q + 1:Q + 2]).then_inc(nrs_done, 1)
                    dve.wait_ge(neg_sum_done, b1)
                    dve.scalar_tensor_tensor(out=Ef[:, 0:1], in0=neg_sum[:, :], scalar=first_eps[:, :],
                                             in1=head_ps[:, Q + 2:Q + 3], op0=ALU.mult,
                                             op1=ALU.add).then_inc(prev_done, 1)
                    dve.scalar_tensor_tensor(out=d_start[:, :], in0=neg_sum[:, :], scalar=-LN_SCALE * CUM_EPS,
                                             in1=head_ps[:, Q:Q + 1], op0=ALU.mult,
                                             op1=ALU.add).then_inc(d_start_done, 1)

                def soft_n(at_slot=0):
                    if not there(SOFT + at_slot):
                        return
                    b1 = batches(turn, u - at_slot)
                    dve.wait_ge(d_start_done, b1)
                    dve.tensor_tensor_scan(D[:, :], E[:, :], E[:, :], d_start[:, :], ALU.add,
                                           ALU.bypass).then_inc(d_done, 1)
                    dve.wait_ge(nrs_done, b1)
                    dve.wait_ge(q_done, b1)
                    dve.wait_ge(d_done, b1)
                    dve.scalar_tensor_tensor(out=Nr, in0=Nr, scalar=nrs[:, :], in1=D[:, :], op0=ALU.mult,
                                             op1=ALU.mult).then_inc(n_done, 1)

                def high_part(at_slot=0):
                    if not there(SOFT + at_slot):
                        return
                    b1 = batches(turn, u - at_slot)
                    dve.wait_ge(rho_done, b1)
                    dve.wait_ge(n_done, b1)
                    if there(SOFT + BATCH + at_slot):
                        at = u - at_slot - BATCH
                        n = turn * (RING // BATCH // 2) + ((at - SOFT) // BATCH // 2 + 1)
                        dve.wait_ge(stacked[at // BATCH % 2], QUARTERS * PARTS * 16 * n)
                    dve.tensor_copy(parts[:, 0, :], both).then_inc(hi_done, 1)

                def mid_part(at_slot=0):
                    if there(SOFT + at_slot):
                        dve.wait_ge(rest_done, batches(turn, u - at_slot))
                        dve.tensor_copy(parts[:, 1, :], left).then_inc(mid_done, 1)

                def low_part(at_slot=0):
                    if there(SOFT + at_slot):
                        dve.wait_ge(mid_done, batches(turn, u - at_slot))
                        dve.tensor_tensor(parts[:, 2, :], left, parts[:, 1, :], ALU.subtract).then_inc(lo_done, 1)

                def scale_wa():
                    if there(STAT):
                        dve.wait_ge(rstd_done, k + 1)
                        dve.tensor_scalar(wa_scaled[u % 2][:, :], wa_sb[:, :], rstd[:, u:u + 1], None,
                                          ALU.mult).then_inc(wa_scaled_done, 1)

                def residual_matrix():
                    if there(STAT):
                        dve.wait_ge(rstd_done, k + 1)
                        dve.scalar_tensor_tensor(out=residual[u][:, :], in0=mat["ident"], scalar=rstd[:, u:u + 1],
                                                 in1=mat["ident"], op0=ALU.mult, op1=ALU.add).then_inc(residual_done, 1)

                def one_plus_square(lag=WIDE):
                    if there(lag):
                        um = (u - lag) % RING
                        dve.wait_ge(wsq_done, 2 * (k - lag) + 2)
                        dve.tensor_scalar(wsq1[um][:, :], wsq[um % 2][:, :], 1.0, None, ALU.add).then_inc(wsq1_done, 1)

                drain = isinstance(k, int) and k >= N
                if u % BATCH == 0 and not drain:
                    times_n(0, lag=PROJ)
                    times_n(1, lag=PROJ)
                    final(1, lag=STORE)
                    group_sum()
                    soft_quotient()
                    soft_floor()
                    running_sum(0)
                    soft_reciprocal()
                    running_sum(1)
                    soft_sums()
                    clamp()
                    final(0)
                    soft_n()
                    scan(0)
                    scan(1)
                    residual_matrix()
                    mid_part()
                    times_n(0)
                elif not drain:
                    group_sum()
                    times_n(1, lag=PROJ)
                    group_mean()
                    low_part(at_slot=1)
                    final(1, lag=STORE)
                    running_sum(0)
                    running_sum(1)
                    soft_max(at_slot=-1)
                    clamp()
                    final(0)
                    scan(0)
                    soft_bias(at_slot=-1)
                    scale_wa()
                    residual_matrix()
                    scan(1)
                    bias_of_w()
                elif u % BATCH == 0:
                    times_n(0, lag=PROJ)
                    soft_floor()
                    times_n(1, lag=PROJ)
                    final(1, lag=STORE)
                    soft_quotient()
                    running_sum(0)
                    soft_reciprocal()
                    running_sum(1)
                    soft_sums()
                    clamp()
                    final(0)
                    soft_n()
                    high_part()
                    scan(0)
                    scan(1)
                    times_n(0)
                    mid_part()
                else:
                    times_n(1, lag=PROJ)
                    final(1, lag=STORE)
                    low_part(at_slot=1)
                    soft_max(at_slot=-1)
                    clamp()
                    scan(0)
                    final(0)
                    one_plus_square()
                    running_sum(1)
                    soft_bias(at_slot=-1)
                    running_sum(0)
                    scan(1)

            run_slots(dve, slot)


def kernel(**inputs):
    import numpy as np
    import concourse.bacc as bacc
    from concourse.bass_utils import run_bass_kernel_spmd

    f = np.float32
    c = np.arange(C)
    eighth, sample, head = c // (HEADS * BATCH), c // HEADS % BATCH, c % HEADS
    same = (sample[:, None] == sample) & (head[:, None] == head)
    made = {
        "ident": c[:, None] == c,
        "group4": c[:, None] // 4 == c // 4,
        "mean_spread": c[:, None] % 32 == c // 4,
        "before": same & (eighth[:, None] < eighth),
        "same": same,
        "neg_same": same * (-1.0 / LN_SCALE),
        "shift": c[:, None] + HEADS * BATCH == c,
    }
    mats = np.stack([made[n].astype(f) for n in MATRICES], axis=1)
    r = np.arange(32)
    sel = np.zeros((PARTS * 32, 2 * BATCH, C), f)
    pick = np.zeros((C, 2 * BATCH, 32), f)
    for odd in range(2):
        for s in range(BATCH):
            mine = (r // (HEADS * BATCH) == odd) & (r // HEADS % BATCH == s)
            row_of = mine & (r % HEADS == c[:, None] // HD)
            pick[:, odd * BATCH + s, :] = row_of
            sel[:, odd * BATCH + s, :] = np.tile(row_of.T, (PARTS, 1))
    group32 = (c[:, None] // 4 == np.arange(GROUPS)).astype(f)
    temp = np.asarray(inputs["L0_conv_temp"]).reshape(HEADS)
    denom_bias = np.asarray(inputs["L0_conv_denom_bias"]).reshape(HEADS)
    chan = np.stack([np.asarray(inputs["L0_conv_ba"]), np.asarray(inputs["L0_conv_bp"]), np.repeat(temp, HD)], axis=1)
    rows = np.concatenate([np.tile(temp, C // HEADS)[:, None], np.tile(denom_bias, C // HEADS)[:, None],
                           (eighth[:, None] == np.arange(EIGHTHS)).astype(f)], axis=1)
    arrays = {
        "x": np.asarray(inputs["x"]),
        "wa_t": np.ascontiguousarray(np.asarray(inputs["L0_conv_Wa"]).T),
        "wp_t": np.ascontiguousarray(np.asarray(inputs["L0_conv_Wp"]).T),
        "chan": np.ascontiguousarray(chan), "rows": np.ascontiguousarray(rows), "mats": np.ascontiguousarray(mats),
        "sel": sel, "pick": pick, "group32": group32,
    }
    nc = bacc.Bacc("TRN2", target_bir_lowering=False, num_devices=1)
    args = [nc.dram_tensor(f"in_{n}", a.shape, mybir.dt.from_np(a.dtype), kind="ExternalInput").ap()
            for n, a in arrays.items()]
    args.append(nc.dram_tensor("out", (N, C, T, V), mybir.dt.float32, kind="ExternalOutput").ap())
    conv_preact(nc, *args)
    r = run_bass_kernel_spmd(nc, [{f"in_{n}": a for n, a in arrays.items()}], core_ids=[0])
    return r.results[0]["out"]
```
